# Optimizing a Trainium2 kernel written in Bass

```python
import numpy as np
import jax
import jax.numpy as jnp

def _softmax(x, axis=-1):
    return jax.nn.softmax(x, axis=axis)

def _gelu(x):
    return jax.nn.gelu(x, approximate=True)

def _silu(x):
    return jax.nn.silu(x)

def _sigmoid(x):
    return jax.nn.sigmoid(x)

def _layernorm(x, axis=-1, eps=1e-05):
    m = jnp.mean(x, axis=axis, keepdims=True)
    v = jnp.var(x, axis=axis, keepdims=True)
    return (x - m) / jnp.sqrt(v + eps)

def _scatter_add(tgt, idx, src, axis=0):
    return tgt.at[idx].add(src)

def _segment_sum(src, seg, n):
    return jax.ops.segment_sum(src, seg, n)
kernel_name = 'mk_xattn_seq_d2_seqx_r4_7c87ec'

def setup_inputs(seed: int=0):
    np.random.seed(seed)
    _w = jnp.asarray

    def _rec_inputs():
        import jax
        import jax.numpy as jnp
        _rk = jax.random.key(seed)
        x = -0.0005146 + 1 * jax.random.normal(jax.random.fold_in(_rk, 1), (8, 256, 512), jnp.float32)
        _lenS = 256 - jax.random.randint(jax.random.fold_in(_rk, 7), (8,), 0, max(1, 256 // 4) + 1, jnp.int32)
        _lenS2 = 256 - jax.random.randint(jax.random.fold_in(_rk, 8), (8,), 0, max(1, 256 // 4) + 1, jnp.int32)
        _ctx_2048P = jax.random.normal(jax.random.fold_in(_rk, 11), (8, 16, 512), jnp.float32)
        _ctx_2048c = jax.random.dirichlet(jax.random.fold_in(_rk, 511), 0.3 * jnp.ones((16,), jnp.float32), (8, 256))
        _ctx_2048t = jnp.einsum('bsk,bkd->bsd', _ctx_2048c, _ctx_2048P)
        _ctx_2048t = _ctx_2048t * jax.lax.rsqrt(jnp.mean(jnp.square(_ctx_2048t)) + 1e-12) * 0.953939
        ctx_2048 = -0.000392918 + 0.999932 * (_ctx_2048t + 0.3 * jax.random.normal(jax.random.fold_in(_rk, 611), (8, 256, 512), jnp.float32))
        _validS = jnp.arange(256)[None, :] < _lenS[:, None]
        _validS2 = jnp.arange(256)[None, :] < _lenS2[:, None]
        _causal = jnp.tril(jnp.ones((256, 256), dtype=bool))
        mask_BxS2_ik0 = jnp.where(jnp.broadcast_to(_validS2[:, :], (8, 256)), 0, 1).astype(jnp.int32)
        return (x, ctx_2048, mask_BxS2_ik0)
    x, ctx_2048, mask_BxS2_ik0 = _rec_inputs()

    def _L0_xattn_setup():
        import jax, jax.numpy as jnp
        import numpy as np
        B, P, K, H, NH = (4, 512, 64, 512, 16)
        DH = H // NH
        EPS = 1e-06

        def rmsnorm(x, w):
            var = jnp.mean(jnp.square(x), axis=-1, keepdims=True)
            return x * jax.lax.rsqrt(var + EPS) * w
        key = jax.random.key(seed)
        ks = jax.random.split(key, 12)
        s = 0.02
        return {'x': jax.random.normal(ks[0], (B, P, H), jnp.float32), 'latents': jax.random.normal(ks[1], (B, K, H), jnp.float32), 'attention_mask': jax.random.randint(ks[2], (B, P), 0, 2, jnp.int32), 'q_w': s * jax.random.normal(ks[3], (H, H), jnp.float32), 'q_b': jnp.zeros((H,), jnp.float32), 'kv_w': s * jax.random.normal(ks[4], (H, 2 * H), jnp.float32), 'kv_b': jnp.zeros((2 * H,), jnp.float32), 'out_w': s * jax.random.normal(ks[5], (H, H), jnp.float32), 'out_b': jnp.zeros((H,), jnp.float32), 'postnorm_w': jnp.ones((H,), jnp.float32), 'mlp_w1': s * jax.random.normal(ks[6], (H, 4 * H), jnp.float32), 'mlp_b1': jnp.zeros((4 * H,), jnp.float32), 'mlp_w2': s * jax.random.normal(ks[7], (4 * H, H), jnp.float32), 'mlp_b2': jnp.zeros((H,), jnp.float32)}
    _L0_xattn_all = _L0_xattn_setup()
    _L0_xattn_in = {k: v for k, v in _L0_xattn_all.items() if k in ('q_w', 'q_b', 'kv_w', 'kv_b', 'out_w', 'out_b', 'postnorm_w', 'mlp_w1', 'mlp_b1', 'mlp_w2', 'mlp_b2')}
    del _L0_xattn_all

    def _L1_xattn_setup():
        import jax, jax.numpy as jnp
        import numpy as np
        B, CQ, CKV, LQ, LKV, HEADS = (4, 256, 256, 512, 512, 16)

        def _conv1x1(W, x):
            return jnp.einsum('oi,bil->bol', W, x)

        def _linear_interp(x, L_out):
            B_, C_, L_in = x.shape
            if L_in == L_out:
                return x
            scale = L_in / L_out
            pos = (jnp.arange(L_out, dtype=x.dtype) + 0.5) * scale - 0.5
            pos = jnp.clip(pos, 0.0, L_in - 1)
            lo = jnp.floor(pos).astype(jnp.int32)
            hi = jnp.minimum(lo + 1, L_in - 1)
            w = pos - lo.astype(x.dtype)
            return x[:, :, lo] * (1.0 - w) + x[:, :, hi] * w
        key = jax.random.key(seed)
        ks = jax.random.split(key, 7)
        winit = 1.0 / np.sqrt(CQ)
        return {'query': jax.random.normal(ks[0], (B, CQ, LQ), dtype=jnp.float32), 'context': jax.random.normal(ks[1], (B, CKV, LKV), dtype=jnp.float32), 'Wq': jax.random.normal(ks[2], (CQ, CQ), dtype=jnp.float32) * winit, 'Wk': jax.random.normal(ks[3], (CQ, CKV), dtype=jnp.float32) * winit, 'Wv': jax.random.normal(ks[4], (CQ, CKV), dtype=jnp.float32) * winit, 'Wo': jax.random.normal(ks[5], (CQ, CQ), dtype=jnp.float32) * winit, 'bo': jnp.zeros((CQ,), dtype=jnp.float32), 'heads': HEADS}
    _L1_xattn_all = _L1_xattn_setup()
    _L1_xattn_in = {k: v for k, v in _L1_xattn_all.items() if k in ('Wq', 'Wk', 'Wv', 'Wo', 'bo')}
    del _L1_xattn_all
    return {'x': x, 'ctx_2048': ctx_2048, 'mask_BxS2_ik0': mask_BxS2_ik0, 'L0_xattn_q_w': _L0_xattn_in['q_w'], 'L0_xattn_q_b': _L0_xattn_in['q_b'], 'L0_xattn_kv_w': _L0_xattn_in['kv_w'], 'L0_xattn_kv_b': _L0_xattn_in['kv_b'], 'L0_xattn_out_w': _L0_xattn_in['out_w'], 'L0_xattn_out_b': _L0_xattn_in['out_b'], 'L0_xattn_postnorm_w': _L0_xattn_in['postnorm_w'], 'L0_xattn_mlp_w1': _L0_xattn_in['mlp_w1'], 'L0_xattn_mlp_b1': _L0_xattn_in['mlp_b1'], 'L0_xattn_mlp_w2': _L0_xattn_in['mlp_w2'], 'L0_xattn_mlp_b2': _L0_xattn_in['mlp_b2'], 'L1_xattn_Wq': _L1_xattn_in['Wq'], 'L1_xattn_Wk': _L1_xattn_in['Wk'], 'L1_xattn_Wv': _L1_xattn_in['Wv'], 'L1_xattn_Wo': _L1_xattn_in['Wo'], 'L1_xattn_bo': _L1_xattn_in['bo']}

def reference(x, ctx_2048, mask_BxS2_ik0, L0_xattn_q_w, L0_xattn_q_b, L0_xattn_kv_w, L0_xattn_kv_b, L0_xattn_out_w, L0_xattn_out_b, L0_xattn_postnorm_w, L0_xattn_mlp_w1, L0_xattn_mlp_b1, L0_xattn_mlp_w2, L0_xattn_mlp_b2, L1_xattn_Wq, L1_xattn_Wk, L1_xattn_Wv, L1_xattn_Wo, L1_xattn_bo):
    import jax
    import jax.numpy as jnp

    def _L0_xattn_ref(x, latents, attention_mask, q_w, q_b, kv_w, kv_b, out_w, out_b, postnorm_w, mlp_w1, mlp_b1, mlp_w2, mlp_b2):
        import jax, jax.numpy as jnp
        import numpy as np
        B, P, K, H, NH = (4, 512, 64, 512, 16)
        DH = H // NH
        EPS = 1e-06

        def rmsnorm(x, w):
            var = jnp.mean(jnp.square(x), axis=-1, keepdims=True)
            return x * jax.lax.rsqrt(var + EPS) * w
        b, p, _ = x.shape
        k_len = latents.shape[1]
        residual = latents
        h = jnp.concatenate([x, latents], axis=1)
        q = (latents @ q_w + q_b).reshape(b, k_len, NH, DH)
        kv = (h @ kv_w + kv_b).reshape(b, p + k_len, NH, DH, 2)
        kmat, v = (kv[..., 0], kv[..., 1])
        attn = jnp.einsum('bkhd,bnhd->bhkn', q, kmat) / DH
        full_mask = jnp.concatenate([attention_mask.astype(bool), jnp.ones((b, k_len), bool)], axis=-1)
        attn = jnp.where(full_mask[:, None, None, :], attn, -jnp.inf)
        attn = jax.nn.softmax(attn.astype(jnp.float32), axis=-1).astype(q.dtype)
        attn_out = jnp.einsum('bhkn,bnhd->bkhd', attn, v).reshape(b, k_len, H)
        attn_out = attn_out @ out_w + out_b + residual
        out = rmsnorm(attn_out, postnorm_w)
        out = jax.nn.gelu(out @ mlp_w1 + mlp_b1) @ mlp_w2 + mlp_b2
        return out + residual

    def _L1_xattn_ref(query, context, Wq, Wk, Wv, Wo, bo, heads):
        import jax, jax.numpy as jnp
        import numpy as np
        B, CQ, CKV, LQ, LKV, HEADS = (4, 256, 256, 512, 512, 16)

        def _conv1x1(W, x):
            return jnp.einsum('oi,bil->bol', W, x)

        def _linear_interp(x, L_out):
            B_, C_, L_in = x.shape
            if L_in == L_out:
                return x
            scale = L_in / L_out
            pos = (jnp.arange(L_out, dtype=x.dtype) + 0.5) * scale - 0.5
            pos = jnp.clip(pos, 0.0, L_in - 1)
            lo = jnp.floor(pos).astype(jnp.int32)
            hi = jnp.minimum(lo + 1, L_in - 1)
            w = pos - lo.astype(x.dtype)
            return x[:, :, lo] * (1.0 - w) + x[:, :, hi] * w
        B_, Cq, Lq = query.shape
        H = heads
        D = Cq // H
        scale = D ** (-0.5)
        q = _conv1x1(Wq, query).reshape(B_, H, D, Lq)
        k = _conv1x1(Wk, context)
        v = _conv1x1(Wv, context)
        if k.shape[2] != Lq:
            k = _linear_interp(k, Lq)
            v = _linear_interp(v, Lq)
        k = k.reshape(B_, H, D, Lq)
        v = v.reshape(B_, H, D, Lq)
        attn = jnp.einsum('bhdi,bhdj->bhij', q, k) * scale
        attn = jax.nn.softmax(attn, axis=-1)
        out = jnp.einsum('bhij,bhdj->bhdi', attn, v).reshape(B_, Cq, Lq)
        return _conv1x1(Wo, out) + bo[None, :, None] + query
    x = _L0_xattn_ref(ctx_2048, x, mask_BxS2_ik0, L0_xattn_q_w, L0_xattn_q_b, L0_xattn_kv_w, L0_xattn_kv_b, L0_xattn_out_w, L0_xattn_out_b, L0_xattn_postnorm_w, L0_xattn_mlp_w1, L0_xattn_mlp_b1, L0_xattn_mlp_w2, L0_xattn_mlp_b2)
    x = _L1_xattn_ref(x, ctx_2048, L1_xattn_Wq, L1_xattn_Wk, L1_xattn_Wv, L1_xattn_Wo, L1_xattn_bo, 16)
    return x

_drawn_inputs = setup_inputs


def setup_inputs(seed=0):
    import zlib

    import numpy as np

    out = dict(_drawn_inputs(seed))
    spreads = {'L0_xattn_q_b': (0.0, 0.8),
     'L0_xattn_kv_b': (0.0, 0.736),
     'L0_xattn_out_b': (0.0, 1.118),
     'L0_xattn_postnorm_w': (1.0, 0.2),
     'L0_xattn_mlp_b1': (0.0, 0.1),
     'L0_xattn_mlp_b2': (0.0, 0.1),
     'L1_xattn_bo': (0.0, 0.1)}
    factors = {'L0_xattn_q_w': 8.0, 'L0_xattn_kv_w': 8.0, 'L0_xattn_out_w': 4.984}
    for name, (base, spread) in spreads.items():
        noise = np.random.default_rng([zlib.crc32(name.encode()), seed]).standard_normal(out[name].shape)
        drawn = base * np.exp(spread * noise) if base else spread * noise
        out[name] = jnp.asarray(drawn.astype(out[name].dtype))
    for name, factor in factors.items():
        out[name] = (out[name] * factor).astype(out[name].dtype)
    return out
```

```python
from contextlib import ExitStack

import concourse.bass as bass
from concourse import mybir

F32 = mybir.dt.float32
F32R = mybir.dt.float32r
I32 = mybir.dt.int32
ALU = mybir.AluOpType
ACT = mybir.ActivationFunctionType
AX_X = mybir.AxisListType.X

P = 128
BANK = 512
MASKED = -1.0e30


def split_product(pe, out, w_hi, w_lo, m_hi, m_lo, first, last):
    pe.matmul(out, w_hi, m_hi, start=first, stop=False)
    pe.matmul(out, w_hi, m_lo, start=False, stop=False)
    return pe.matmul(out, w_lo, m_hi, start=False, stop=last)


def wait_apart(eng, started, *waits):
    values = [value if isinstance(value, int) else eng.to_reg(value) for _, value in waits]
    eng.wait_ge(started, 1)
    for (sem, _), value in zip(waits, values):
        eng.wait_ge(sem, value)


def attention0(nc, psum, latents, hT, mask, w_q, w_k, w_v, w_out, b_qkv, b_out, y_mid):
    B, LAT, F = latents.shape
    KEYS = hT.shape[2]
    FT = F // P
    KT = KEYS // P
    QT = LAT // P
    D = 32
    HPG = P // D
    UNITS = B * FT
    SCALE = 1.0 / D
    RING = 4
    AHEAD = 3
    TURN = 2 * FT
    TURNS = B // 2
    QK = LAT + KEYS
    GEN = (4, 5, 6)
    OBANK = 7
    PT_HEADS = 2 * HPG

    with ExitStack() as ctx:
        def sb(name, shape, dt=F32):
            return ctx.enter_context(nc.sbuf_tensor("a0_" + name, shape, dt))

        def sem(name):
            return ctx.enter_context(nc.semaphore("a0_" + name))

        W_hi = sb("W_hi", [P, 4, FT, F], F32R)
        W_lo = sb("W_lo", [P, 4, FT, F], F32R)
        QKS = sb("QKS", [P, RING, HPG, QK], F32R)
        PT = sb("PT", [P, PT_HEADS, KT * LAT])
        V = sb("V", [P, 2, KT, F])
        hT_hi = sb("hT_hi", [P, FT, KEYS], F32R)
        hT_lo = sb("hT_lo", [P, FT, KEYS], F32R)
        stage = sb("stage", [P, 2, KEYS])
        OT_hi = sb("OT_hi", [P, FT, LAT], F32R)
        OT_lo = sb("OT_lo", [P, FT, LAT], F32R)
        srcA = sb("srcA", [P, QK], F32R)
        srcB = sb("srcB", [P, QK], F32R)
        srcC = sb("srcC", [P, QK], F32R)
        xb = sb("xb", [P, QT, F])
        bo = sb("bo", [P, F])
        ident = sb("ident", [P, P])
        ones = sb("ones", [P, D])
        bias = sb("bias", [P, 3, FT])
        rsum = sb("rsum", [P, LAT])
        oscaled = sb("oscaled", [P, LAT])
        mx = sb("mx", [P, QT, HPG])
        mrow = sb("mrow", [HPG, LAT], F32R)
        mask_d = nc.dram_tensor("mask_rows", (B, 1, HPG, KEYS), F32, kind="Internal").ap()

        with ExitStack() as c0:
            def sem0(name):
                return c0.enter_context(nc.semaphore("a0p_" + name))

            mask_i = xb[0:B, 0, 0:LAT].bitcast(I32)
            mask_r = bo[0:B, :]
            w_loaded = [sem0(f"w_loaded{m}") for m in range(4)]
            small_loaded = sem0("small_loaded")
            bo_loaded = sem0("bo_loaded")
            w_hi_done = sem0("w_hi_done")
            zeroed = sem0("zeroed")
            masked = sem0("masked")
            mask_stored = sem0("mask_stored")
            stagew = PT[:, :, :].rearrange("p (m s) n -> p m (s n)", m=4)
            block = c0.enter_context(nc.Block())

            @block.sync
            def _(sp):
                for m, w in enumerate((w_q, w_k, w_v, w_out)):
                    sp.dma_start(stagew[:, m, :].rearrange("p (t n) -> p t n", t=FT),
                                 w.rearrange("(t p) n -> p t n", p=P)).then_inc(w_loaded[m], 16)
                    if m == 0:
                        sp.dma_start(mask_i, mask).then_inc(small_loaded, 16)
                        sp.dma_start(bias[:, :, :], b_qkv).then_inc(small_loaded, 16)
                sp.wait_ge(masked, 2)
                for j in range(HPG):
                    sp.dma_start(mask_d[:, 0, j, :], mask_r).then_inc(mask_stored, 16)
                sp.wait_ge(mask_stored, 16 * HPG)
                sp.dma_start(bo[:, :], b_out.to_broadcast((P, F))).then_inc(bo_loaded, 16)
                sp.wait_ge(bo_loaded, 16)
                sp.wait_ge(small_loaded, 32)

            @block.scalar
            def _(act):
                for m in range(4):
                    act.wait_ge(w_loaded[m], 16)
                    act.activation(W_hi[:, m, :, :], stagew[:, m, :].rearrange("p (t n) -> p t n", t=FT),
                                   ACT.Copy).then_inc(w_hi_done, 1)

            @block.vector
            def _(dve):
                dve.memset(mask_r, 0.0).then_inc(masked, 1)
                dve.memset(QKS[96:98, :, :, :].bitcast(F32), 1.0)
                dve.memset(ones[:, :], 1.0)
                dve.wait_ge(masked, 1)
                dve.wait_ge(small_loaded, 32)
                dve.tensor_scalar(mask_r[:, 0:KEYS - LAT], mask_i, 0.0, MASKED, ALU.is_equal,
                                  ALU.mult).then_inc(masked, 1)
                for m in range(4):
                    dve.wait_ge(w_hi_done, m + 1)
                    dve.tensor_tensor(W_lo[:, m, :, :], stagew[:, m, :].rearrange("p (t n) -> p t n", t=FT),
                                      W_hi[:, m, :, :].bitcast(F32), ALU.subtract)

            @block.gpsimd
            def _(pool):
                pool.memset(ident[:, :], 0.0).then_inc(zeroed, 1)
                pool.wait_ge(zeroed, 1)
                pool.affine_select(out=ident[:, :], in_=ident[:, :], compare_op=ALU.not_equal, fill=1.0,
                                   base=0, pattern=[[-1, P]], channel_multiplier=1)

        gen_filled = sem("gen_filled")
        gen_released = sem("gen_released")
        ht_loaded = [sem("ht_loaded0"), sem("ht_loaded1")]
        ht_hi = sem("ht_hi")
        ht_lo = sem("ht_lo")
        qk_hi = sem("qk_hi")
        qk_copied = sem("qk_copied")
        stack_loaded = [sem(f"stack_loaded{r}") for r in range(RING)]
        max_loaded = sem("max_loaded")
        st_filled = sem("st_filled")
        exp_done = sem("exp_done")
        av_done = sem("av_done")
        recip_done = sem("recip_done")
        o_scaled = sem("o_scaled")
        o_hi = sem("o_hi")
        o_lo = sem("o_lo")
        x_loaded = [sem(f"x_loaded{t}") for t in range(QT)]
        bo_added = sem("bo_added")
        y_stored = [sem(f"y_stored{t}") for t in range(QT)]
        mask_loaded = [sem(f"mask_loaded{r}") for r in range(RING)]
        STACK = 16 * 3 * HPG

        PROLOGUE = [("HT", 0, ft) for ft in range(FT)]
        PROLOGUE += [("Q", 0, 0), ("K", 0, 0), ("V", 0, 0), ("V", 0, 1), ("Q", 1, 0), ("K", 1, 0)]
        PROLOGUE += [("S", 0, j) for j in range(HPG)] + [("M", 0, 0)]
        PROLOGUE += [("V", 0, 2), ("V", 0, 3), ("Q", 2, 0), ("K", 2, 0)]

        def step(lu, last):
            g = lu % FT
            score = not (last and lu == TURN - 1)
            project = not (last and lu + AHEAD >= TURN)
            more = not (last and lu >= FT)
            out = []
            for j in range(HPG):
                out += [("ST", lu, j)]
                out += [("S", lu + 1, j)] * score
                if j == 1:
                    out += [("Q", lu + AHEAD, 0)] * project
            rows = [("HT", lu // FT + 1, ft) for ft in range(FT)] * (more and g == 0)
            out += [("K", lu + AHEAD, 0)] * project + [("M", lu + 1, 0)] * score
            out += rows[:2] + [("AV", lu, 0)] + rows[2:]
            if more:
                out += [("V", lu // FT + 1, n) for n in ((), (0,), (1, 2), (3,))[g]]
            if g == FT - 1:
                out += [("OUT", lu // FT, t) for t in range(QT)]
            return out

        USES = {"S": QT, "Q": 1, "K": 1, "M": 1, "V": 1, "OUT": 1}

        def counted(stages, n):
            out = []
            for stage in stages:
                out.append((*stage, n))
                n += USES.get(stage[0], 0)
            return out, n

        prologue, N0 = counted(PROLOGUE, 0)
        turn, n_end = counted([s for lu in range(TURN) for s in step(lu, False)], N0)
        last_turn, _ = counted([s for lu in range(TURN) for s in step(lu, True)], N0)
        PER_TURN = n_end - N0
        LAST = TURNS - 1

        def walk(eng, stage_of):
            stage_of(0, prologue)
            with eng.Fori(0, LAST) as t:
                stage_of(t, turn)
            stage_of(LAST, last_turn)

        started = [sem("pool_started"), sem("sp_started")]

        block = ctx.enter_context(nc.Block())

        @block.tensor
        def _(pe):
            def claim(t, n):
                free = n - len(GEN) + 1
                if n >= N0 and n - N0 < len(GEN):
                    free = N0
                if free > 0:
                    pe.wait_ge(gen_released, t * PER_TURN + free)
                return GEN[n % len(GEN)]

            def stages(t, todo):
                first_s = {}
                for kind, lv, x, n in todo:
                    slot, g, b = lv % RING, lv % FT, lv // FT
                    if kind in ("Q", "K", "V") and (kind != "V" or x == 0):
                        bb = b if kind != "V" else lv
                        pe.wait_ge(ht_lo, t * (2 * FT) + FT * (bb + 1))
                    if kind in ("Q", "K"):
                        m, cols = (0, slice(KEYS - LAT, KEYS)) if kind == "Q" else (1, slice(0, KEYS))
                        bank = claim(t, n)
                        for ft in range(FT):
                            fs = slice(g * P, (g + 1) * P)
                            mm = split_product(pe, psum[:, bank, 0:cols.stop - cols.start],
                                               W_hi[:, m, ft, fs], W_lo[:, m, ft, fs],
                                               hT_hi[:, ft, cols], hT_lo[:, ft, cols],
                                               ft == 0, ft == FT - 1)
                        mm.then_inc(gen_filled, 1)
                    if kind == "V":
                        bank = claim(t, n)
                        for ft in range(FT):
                            ks = slice(x * P, (x + 1) * P)
                            mm = split_product(pe, psum[:, bank, :], hT_hi[:, ft, ks], hT_lo[:, ft, ks],
                                               W_hi[:, 2, ft, :], W_lo[:, 2, ft, :],
                                               ft == 0, ft == FT - 1)
                        mm.then_inc(gen_filled, 1)
                    if kind == "S":
                        if x == 0:
                            pe.wait_ge(stack_loaded[slot], t * (TURN // RING * STACK)
                                       + (lv // RING + 1) * STACK)
                            pe.wait_ge(mask_loaded[slot], t * (TURN // RING * 16) + (lv // RING + 1) * 16)
                        for q in range(QT):
                            bank = claim(t, n + q)
                            pe.matmul(psum[:, bank, :], QKS[0:97, slot, x, q * P:(q + 1) * P],
                                      QKS[0:97, slot, x, LAT:QK], start=True,
                                      stop=True).then_inc(gen_filled, 1)
                    if kind == "M":
                        last_s = max(m for k, v, _, m in todo if k == "S" and v == lv) + QT
                        pe.wait_ge(gen_released, t * PER_TURN + last_s)
                        bank = claim(t, n)
                        for q in range(QT):
                            mm = pe.transpose(psum[0:HPG, bank, q * P:(q + 1) * P], mx[:, q, :],
                                              ident[:, :])
                        mm.then_inc(gen_filled, 1)
                    if kind == "ST":
                        h = HPG * lv + x
                        if x == 0:
                            pe.wait_ge(max_loaded, t * (16 * TURN) + 16 * (lv + 1))
                        pe.wait_ge(exp_done, t * (TURN * HPG) + h + 1)
                        for kt in range(KT):
                            at = (h % 2) * KT * LAT + kt * LAT
                            mm = pe.matmul(psum[:, at // BANK, at % BANK:at % BANK + LAT],
                                           QKS[0:98, slot, x, LAT + kt * P:LAT + (kt + 1) * P],
                                           QKS[0:98, slot, x, 0:LAT], start=True, stop=True)
                        mm.then_inc(st_filled, 1)
                    if kind == "AV":
                        pe.wait_ge(exp_done, t * (TURN * HPG) + HPG * (lv + 1) + 2)
                        pe.wait_ge(o_scaled, t * TURN + lv + 1)
                        for kt in range(KT):
                            for j in range(HPG):
                                rows = slice(j * D, (j + 1) * D)
                                pt = PT[:, (HPG * lv + j) % PT_HEADS, kt * LAT:(kt + 1) * LAT]
                                f0 = g * P + j * D
                                pe.matmul(psum[rows, OBANK, 0:LAT], V[:, b % 2, kt, f0:f0 + D], pt,
                                          start=(kt == 0), stop=(kt == KT - 1), skip_group_check=True)
                        for kt in range(KT):
                            for j in range(HPG):
                                rows = slice(j * D, (j + 1) * D)
                                pt = PT[:, (HPG * lv + j) % PT_HEADS, kt * LAT:(kt + 1) * LAT]
                                mm = pe.matmul(psum[rows, OBANK, LAT:2 * LAT], ones[:, :], pt,
                                               start=False, stop=(kt == KT - 1), skip_group_check=True)
                        mm.then_inc(av_done, 1)
                    if kind == "OUT":
                        if x == 0:
                            pe.wait_ge(o_lo, t * TURN + FT * (lv + 1) + 1)
                        bank = claim(t, n)
                        for ft in range(FT):
                            ls = slice(x * P, (x + 1) * P)
                            mm = split_product(pe, psum[:, bank, :], OT_hi[:, ft, ls], OT_lo[:, ft, ls],
                                               W_hi[:, 3, ft, :], W_lo[:, 3, ft, :],
                                               ft == 0, ft == FT - 1)
                        mm.then_inc(gen_filled, 1)

            pe.sem_inc(av_done, 2)
            pe.sem_inc(st_filled, 1)
            walk(pe, stages)

        @block.scalar
        def _(act):
            def stages(t, todo):
                for kind, lv, x, n in todo:
                    slot, g = lv % RING, lv % FT
                    if kind == "HT":
                        act.wait_ge(ht_loaded[x % 2], t * (16 * FT) + 16 * (FT // 2 * lv + x // 2 + 1))
                        act.activation(hT_hi[:, x, :], stage[:, x % 2, :], ACT.Copy).then_inc(ht_hi, 1)
                    if kind in ("Q", "K"):
                        act.wait_ge(gen_filled, t * PER_TURN + n + 1)
                        if kind == "Q" and (lv >= 1):
                            act.wait_ge(stack_loaded[(lv - 1) % RING], t * (TURN // RING * STACK)
                                        + ((lv - 1) // RING + 1) * STACK)
                        m, cols = (0, slice(0, LAT)) if kind == "Q" else (1, slice(LAT, QK))
                        act.activation(srcA[:, cols], psum[:, GEN[n % len(GEN)], 0:cols.stop - cols.start],
                                       ACT.Identity, bias=bias[:, m, g:g + 1]).then_inc(qk_hi, 1)
                    if kind == "ST":
                        h = HPG * lv + x
                        act.wait_ge(st_filled, t * (TURN * HPG) + h + 1 + 1)
                        if x == 0:
                            act.wait_ge(av_done, t * TURN + lv + 1)
                        act.activation(PT[:, h % PT_HEADS, :],
                                       psum[:, (h % 2) * 2:(h % 2) * 2 + 2, :].rearrange("p s n -> p (s n)"),
                                       ACT.Exp, scale=SCALE).then_inc(exp_done, 1)
                    if kind == "AV":
                        act.wait_ge(o_scaled, t * TURN + lv + 1 + 1)
                        act.activation(OT_hi[:, g, :], oscaled[:, :], ACT.Identity,
                                       bias=bias[:, 2, g:g + 1]).then_inc(o_hi, 1)

            act.sem_inc(exp_done, 2)
            walk(act, stages)

        @block.vector
        def _(dve):
            def stages(t, todo):
                for kind, lv, x, n in todo:
                    g = lv % FT
                    bank = GEN[n % len(GEN)]
                    if kind == "HT":
                        dve.wait_ge(ht_hi, t * (2 * FT) + FT * lv + x + 1)
                        dve.tensor_tensor(hT_lo[:, x, :], stage[:, x % 2, :], hT_hi[:, x, :].bitcast(F32),
                                          ALU.subtract).then_inc(ht_lo, 1)
                    if kind in ("Q", "K"):
                        dve.wait_ge(qk_hi, t * (2 * TURN) + 2 * lv + (1 if kind == "Q" else 2))
                        m, cols, lo = (0, slice(0, LAT), srcC) if kind == "Q" else (1, slice(LAT, QK), srcB)
                        dve.scalar_tensor_tensor(out=lo[:, cols], in0=psum[:, bank, 0:cols.stop - cols.start],
                                                 scalar=bias[:, m, g:g + 1], in1=srcA[:, cols].bitcast(F32),
                                                 op0=ALU.add, op1=ALU.subtract).then_inc(gen_released, 1)
                    if kind == "V":
                        dve.wait_ge(gen_filled, t * PER_TURN + n + 1)
                        dve.tensor_copy(V[:, lv % 2, x, :], psum[:, bank, :]).then_inc(gen_released, 1)
                    if kind == "S":
                        for q in range(QT):
                            dve.wait_ge(gen_filled, t * PER_TURN + n + q + 1)
                            dve.tensor_reduce(mx[:, q, x:x + 1], psum[:, GEN[(n + q) % len(GEN)], :], AX_X,
                                              ALU.max).then_inc(gen_released, 1)
                    if kind == "M":
                        dve.wait_ge(gen_filled, t * PER_TURN + n + 1)
                        if lv > 0:
                            dve.wait_ge(max_loaded, t * (16 * TURN) + 16 * lv)
                        dve.tensor_scalar(mrow[:, :], psum[0:HPG, bank, 0:LAT], -1.0, None,
                                          ALU.mult).then_inc(gen_released, 1)
                    if kind == "AV":
                        dve.wait_ge(av_done, t * TURN + lv + 1 + 2)
                        dve.wait_ge(o_lo, t * TURN + lv + 1)
                        dve.reciprocal(rsum[:, :], psum[:, OBANK, LAT:2 * LAT]).then_inc(recip_done, 1)
                        dve.wait_ge(recip_done, t * TURN + lv + 1)
                        dve.tensor_tensor(oscaled[:, :], psum[:, OBANK, 0:LAT], rsum[:, :],
                                          ALU.mult).then_inc(o_scaled, 1)
                        dve.wait_ge(o_hi, t * TURN + lv + 1)
                        dve.scalar_tensor_tensor(out=OT_lo[:, g, :], in0=oscaled[:, :],
                                                 scalar=bias[:, 2, g:g + 1], in1=OT_hi[:, g, :].bitcast(F32),
                                                 op0=ALU.add, op1=ALU.subtract).then_inc(o_lo, 1)
                    if kind == "OUT":
                        dve.wait_ge(gen_filled, t * PER_TURN + n + 1)
                        dve.wait_ge(bo_added, t * (2 * QT) + QT * lv + x + 1)
                        dve.tensor_tensor(xb[:, x, :], psum[:, bank, :], xb[:, x, :],
                                          ALU.add).then_inc(gen_released, 1)

            dve.sem_inc(o_scaled, 1)
            dve.sem_inc(o_lo, 1)
            walk(dve, stages)

        @block.gpsimd
        def _(pool):
            def stages(t, todo):
                for kind, lv, x, n in todo:
                    slot, b = lv % RING, lv // FT
                    if kind in ("Q", "K"):
                        wait_apart(pool, started[0],
                                   (qk_hi, t * (2 * TURN) + 2 * lv + (1 if kind == "Q" else 2)))
                        cols, copy = (slice(0, LAT), srcB) if kind == "Q" else (slice(LAT, QK), srcC)
                        pool.tensor_copy(copy[:, cols], srcA[:, cols]).then_inc(qk_copied, 1)
                    if kind == "Q":
                        if lv >= RING - 1:
                            wait_apart(pool, started[0],
                                       (st_filled, t * (TURN * HPG) + HPG * (lv - RING + 1) + 1))
                        pool.dma_start(QKS[96:97, slot, :, LAT:QK].bitcast(F32),
                                       mask_d[t * 2 + b]).then_inc(mask_loaded[slot], 16)
                    if kind == "AV" and lv % FT in (2, 3):
                        q = lv % FT - 2
                        pool.wait_ge(x_loaded[q], t * 32 + 16 * (b + 1))
                        pool.tensor_tensor(xb[:, q, :], xb[:, q, :], bo[:, :], ALU.add).then_inc(bo_added, 1)

            pool.sem_inc(started[0], 1)
            walk(pool, stages)

        @block.sync
        def _(sp):
            def load_rows(t, b, ft):
                if not (isinstance(t, int) and t * 2 + b == 0 and ft < 2):
                    sp.wait_ge(ht_lo, t * (2 * FT) + FT * b + ft - 1)
                sp.dma_start(stage[:, ft % 2, :],
                             hT[t * 2 + b, ft * P:(ft + 1) * P, :]).then_inc(ht_loaded[ft % 2], 16)

            def stages(t, todo):
                order = list(todo)
                for m in range(1, len(order)):
                    if order[m][0] == "M" and order[m - 1][0] == "K":
                        order[m - 1:m + 1] = order[m], order[m - 1]
                for kind, lv, x, n in order:
                    slot, g, b = lv % RING, lv % FT, lv // FT
                    if kind == "HT" and (x >= 2 or (isinstance(t, int) and t * 2 + lv == 0)):
                        load_rows(t, lv, x)
                    if kind == "K":
                        waits = [(qk_copied, t * (2 * TURN) + 2 * (lv + 1)),
                                 (gen_released, t * PER_TURN + n + 1)]
                        if lv >= RING - 1:
                            waits.append((st_filled, t * (TURN * HPG) + HPG * (lv - RING + 1) + 1))
                        wait_apart(sp, started[1], *waits)
                        for j in range(HPG):
                            rows = slice(j * D, (j + 1) * D)
                            for r, src in enumerate((srcA, srcB, srcC)):
                                sp.dma_start(QKS[r * D:(r + 1) * D, slot, j, :].bitcast(F32),
                                             src[rows, :].bitcast(F32)).then_inc(stack_loaded[slot], 16)
                    if kind == "M":
                        sp.wait_ge(gen_released, t * PER_TURN + n + 1)
                        sp.dma_start(QKS[97:98, slot, :, 0:LAT].bitcast(F32),
                                     mrow[:, :].bitcast(F32)).then_inc(max_loaded, 16)
                        if isinstance(t, int) and t * TURN + lv == 0:
                            for ft in range(2):
                                load_rows(t, 1, ft)
                    if kind == "AV" and g in (1, 2):
                        q = g - 1
                        sp.wait_ge(y_stored[q], t * 32 + 16 * b + 16)
                        sp.dma_start(xb[:, q, :], latents[t * 2 + b, q * P:(q + 1) * P, :])\
                            .then_inc(x_loaded[q], 16)
                    if kind == "OUT":
                        sp.wait_ge(gen_released, t * PER_TURN + n + 1)
                        sp.dma_start(y_mid[t * 2 + lv, x * P:(x + 1) * P, :], xb[:, x, :])\
                            .then_inc(y_stored[x], 16)
                        if x == 1 and not (isinstance(t, int) and t * 2 + lv >= B - 2):
                            for ft in range(2):
                                load_rows(t, lv + 2, ft)

            sp.sem_inc(started[1], 1)
            for q in range(QT):
                sp.sem_inc(y_stored[q], 16)
            walk(sp, stages)
            for q in range(QT):
                sp.wait_ge(y_stored[q], 16 * B + 16)


def mlp(nc, psum, y_mid, latents, w1, w2, b1, b2, norm_w, y_out):
    B, LAT, F = latents.shape
    HID = w1.shape[1]
    FT = F // P
    HT = HID // P
    QT = LAT // P
    PAIRS = B // 2
    TT = 2 * QT
    TOK = TT * P
    AHEAD = 2
    CHUNK = 2 * P
    CHUNKS = HID // CHUNK
    G = 4
    EPS = 1e-6
    M1_BANK, T_BANK, ACC = 0, 2, 4

    with ExitStack() as ctx:
        def sb(name, shape, dt=F32):
            return ctx.enter_context(nc.sbuf_tensor("m_" + name, shape, dt))

        def sem(name):
            return ctx.enter_context(nc.semaphore("m_" + name))

        W1_hi = sb("W1_hi", [P, FT, HID], F32R)
        W1_lo = sb("W1_lo", [P, FT, HID], F32R)
        W2_hi = sb("W2_hi", [P, HT, F], F32R)
        W2_lo = sb("W2_lo", [P, HT, F], F32R)
        stage1 = sb("stage1", [P, 2, FT, CHUNK])
        stage2 = sb("stage2", [P, 2, CHUNK // P, F])
        xt = sb("xt", [P, TT, F])
        square = sb("square", [P, QT, F])
        nT_hi = sb("nT_hi", [P, FT, TOK], F32R)
        nT_lo = sb("nT_lo", [P, FT, TOK], F32R)
        g = sb("g", [P, 2, TOK])
        g_hi = sb("g_hi", [P, G, TOK], F32R)
        g_lo = sb("g_lo", [P, G, TOK], F32R)
        res = sb("res", [P, TT, F])
        b2_rows = sb("b2_rows", [P, F])
        b1_col = sb("b1_col", [P, HT])
        norm_col = sb("norm_col", [P, FT])
        ident = sb("ident", [P, P])
        mean = sb("mean", [P, TT])
        root = sb("root", [P, TT])
        r0 = sb("r0", [P, TT])
        corr = sb("corr", [P, TT])
        rstd = sb("rstd", [P, TT])

        const_loaded = sem("const_loaded")
        ident_zero = sem("ident_zero")
        ident_ready = sem("ident_ready")
        w_loaded = [sem("w_loaded0"), sem("w_loaded1")]
        w_hi = sem("w_hi")
        w_lo = sem("w_lo")
        x_loaded = sem("x_loaded")
        res_loaded = sem("res_loaded")
        res_ready = sem("res_ready")
        stat = sem("stat")
        rooted = sem("rooted")
        normed = sem("normed")
        t_filled = sem("t_filled")
        t_hi = sem("t_hi")
        t_lo = sem("t_lo")
        m1_filled = sem("m1_filled")
        gelu_done = sem("gelu_done")
        g_hi_done = sem("g_hi_done")
        g_lo_done = sem("g_lo_done")
        m2_done = sem("m2_done")
        acc_filled = sem("acc_filled")
        acc_read = sem("acc_read")
        y_stored = sem("y_stored")
        started = sem("started")

        def pair_stages(first, last):
            out = []
            if first:
                out += [("W", 0), ("W", 1), ("L", -1), ("N", -1)]
                out += [("T", ft - FT) for ft in range(FT)] + [("M1", 0), ("M1", 1)]
            for f in range(HT):
                if first and f % 2 == 0 and f // 2 + 2 < CHUNKS:
                    out += [("W", f // 2 + 2)]
                if f == 1 and not last:
                    out += [("L", 0)]
                if f == 2:
                    out += [("R", 0)]
                if f == 6 and not last:
                    out += [("N", 0)]
                if f >= HT - 2 and not last:
                    out += [("T", 2 * (f - HT + 2)), ("T", 2 * (f - HT + 2) + 1)]
                out += [("M2", f)]
                if f + AHEAD < HT:
                    out += [("M1", f + AHEAD)]
            if not last:
                out += [("M1", HT), ("M1", HT + 1)]
            return out

        def walk(eng, stage_of):
            stage_of(0, pair_stages(True, False))
            with eng.Fori(1, PAIRS - 1) as t:
                stage_of(t, pair_stages(False, False))
            stage_of(PAIRS - 1, pair_stages(False, True))

        STATS = 11

        block = ctx.enter_context(nc.Block())

        @block.tensor
        def _(pe):
            def stages(t, todo):
                for kind, x in todo:
                    if kind == "T":
                        ft = x % FT
                        if x == -FT:
                            pe.wait_ge(ident_ready, 1)
                        if ft == 0:
                            pe.wait_ge(normed, t * TT + (TT if x < 0 else 2 * TT))
                        pe.wait_ge(t_lo, t * FT + x + FT + 1)
                        for i in range(TT):
                            mm = pe.transpose(psum[:, T_BANK + ft % 2, i * P:(i + 1) * P],
                                              xt[:, i, ft * P:(ft + 1) * P], ident[:, :])
                        mm.then_inc(t_filled, 1)
                    if kind == "M1":
                        f = x % HT
                        if x % HT == 0:
                            pe.wait_ge(t_lo, t * FT + FT * (x // HT + 1) + 2)
                        if isinstance(t, int) and t == 0 and x < HT and x % 2 == 0:
                            pe.wait_ge(w_lo, 2 * (x // 2 + 1))
                        pe.wait_ge(gelu_done, t * HT + x + 1)
                        fs = slice(f * P, (f + 1) * P)
                        for ft in range(FT):
                            mm = split_product(pe, psum[:, M1_BANK + x % 2, :],
                                               W1_hi[:, ft, fs], W1_lo[:, ft, fs],
                                               nT_hi[:, ft, :], nT_lo[:, ft, :], ft == 0, ft == FT - 1)
                        mm.then_inc(m1_filled, 1)
                    if kind == "M2":
                        pe.wait_ge(g_lo_done, t * HT + x + 1 + 2)
                        for i in range(TT):
                            if x == 0:
                                pe.wait_ge(acc_read, t * TT + i + 1)
                            ts = slice(i * P, (i + 1) * P)
                            mm = split_product(pe, psum[:, ACC + i, :], g_hi[:, x % G, ts], g_lo[:, x % G, ts],
                                               W2_hi[:, x, :], W2_lo[:, x, :], x == 0, x == HT - 1)
                            if x == HT - 1:
                                mm.then_inc(acc_filled, 1)
                        if x < HT - 1:
                            mm.then_inc(m2_done, 1)
                        else:
                            pe.wait_ge(acc_filled, t * TT + TT)
                            pe.sem_inc(m2_done, 1)

            pe.sem_inc(m2_done, G)
            walk(pe, stages)

        @block.scalar
        def _(act):
            act.wait_ge(const_loaded, 48)

            def stages(t, todo):
                for kind, x in todo:
                    if kind == "W":
                        act.wait_ge(w_loaded[x % 2], 32 * (x // 2 + 1))
                        act.activation(W1_hi[:, :, x * CHUNK:(x + 1) * CHUNK], stage1[:, x % 2, :, :],
                                       ACT.Copy).then_inc(w_hi, 1)
                        act.activation(W2_hi[:, 2 * x:2 * x + 2, :], stage2[:, x % 2, :, :],
                                       ACT.Copy).then_inc(w_hi, 1)
                    if kind == "N":
                        act.wait_ge(stat, t * STATS + STATS * (x + 1) + 5)
                        act.activation(root[:, :], mean[:, :], ACT.Sqrt).then_inc(rooted, 1)
                    if kind == "T":
                        ft = x % FT
                        act.wait_ge(t_filled, t * FT + x + FT + 1)
                        act.activation(nT_hi[:, ft, :], psum[:, T_BANK + ft % 2, :], ACT.Identity,
                                       scale=norm_col[:, ft:ft + 1]).then_inc(t_hi, 1)
                    if kind == "M1":
                        act.wait_ge(m1_filled, t * HT + x + 1)
                        act.wait_ge(g_lo_done, t * HT + x + 1)
                        act.activation(g[:, x % 2, :], psum[:, M1_BANK + x % 2, :], ACT.Gelu_apprx_tanh,
                                       bias=b1_col[:, x % HT:x % HT + 1]).then_inc(gelu_done, 1)
                        act.wait_ge(gelu_done, t * HT + x + 1 + 2)
                        act.wait_ge(m2_done, t * HT + x + 1)
                        act.activation(g_hi[:, x % G, :], g[:, x % 2, :], ACT.Copy).then_inc(g_hi_done, 1)

            act.sem_inc(gelu_done, 2)
            walk(act, stages)

        @block.vector
        def _(dve):
            dve.wait_ge(const_loaded, 48)

            def stages(t, todo):
                for kind, x in todo:
                    if kind == "W":
                        dve.wait_ge(w_hi, 2 * x + 1)
                        cs = slice(x * CHUNK, (x + 1) * CHUNK)
                        dve.tensor_tensor(W1_lo[:, :, cs], stage1[:, x % 2, :, :],
                                          W1_hi[:, :, cs].bitcast(F32), ALU.subtract).then_inc(w_lo, 1)
                        dve.wait_ge(w_hi, 2 * x + 2)
                        dve.tensor_tensor(W2_lo[:, 2 * x:2 * x + 2, :], stage2[:, x % 2, :, :],
                                          W2_hi[:, 2 * x:2 * x + 2, :].bitcast(F32),
                                          ALU.subtract).then_inc(w_lo, 1)
                    if kind == "N":
                        p = x + 1
                        s = t * STATS + STATS * p
                        for b in range(2):
                            dve.wait_ge(x_loaded, t * 32 + 32 * p + 32)
                            if b == 1:
                                dve.wait_ge(stat, s + 2)
                            bs = slice(QT * b, QT * (b + 1))
                            dve.tensor_tensor(square[:, :, :], xt[:, bs, :], xt[:, bs, :],
                                              ALU.mult).then_inc(stat, 1)
                            dve.wait_ge(stat, s + 2 * b + 1)
                            dve.tensor_reduce(mean[:, bs], square[:, :, :], AX_X, ALU.add).then_inc(stat, 1)
                        dve.wait_ge(stat, s + 4)
                        dve.tensor_scalar(mean[:, :], mean[:, :], 1.0 / F, EPS, ALU.mult,
                                          ALU.add).then_inc(stat, 1)
                        dve.wait_ge(rooted, t + p + 1)
                        dve.reciprocal(r0[:, :], root[:, :]).then_inc(stat, 1)
                        dve.wait_ge(stat, s + 6)
                        dve.tensor_tensor(corr[:, :], mean[:, :], r0[:, :], ALU.mult).then_inc(stat, 1)
                        dve.wait_ge(stat, s + 7)
                        dve.tensor_tensor(corr[:, :], corr[:, :], r0[:, :], ALU.mult).then_inc(stat, 1)
                        dve.wait_ge(stat, s + 8)
                        dve.tensor_scalar(corr[:, :], corr[:, :], -0.5, 1.5, ALU.mult,
                                          ALU.add).then_inc(stat, 1)
                        dve.wait_ge(stat, s + 9)
                        dve.tensor_tensor(rstd[:, :], r0[:, :], corr[:, :], ALU.mult).then_inc(stat, 1)
                        dve.wait_ge(stat, s + 10)
                        for i in range(TT):
                            dve.tensor_scalar(xt[:, i, :], xt[:, i, :], rstd[:, i:i + 1], None,
                                              ALU.mult).then_inc(normed, 1)
                        dve.wait_ge(normed, t * TT + TT * (p + 1))
                        dve.sem_inc(stat, 1)
                    if kind == "T":
                        ft = x % FT
                        dve.wait_ge(t_hi, t * FT + x + FT + 1)
                        dve.scalar_tensor_tensor(out=nT_lo[:, ft, :], in0=psum[:, T_BANK + ft % 2, :],
                                                 scalar=norm_col[:, ft:ft + 1],
                                                 in1=nT_hi[:, ft, :].bitcast(F32), op0=ALU.mult,
                                                 op1=ALU.subtract).then_inc(t_lo, 1)
                    if kind == "M1":
                        dve.wait_ge(g_hi_done, t * HT + x + 1)
                        dve.tensor_tensor(g_lo[:, x % G, :], g[:, x % 2, :],
                                          g_hi[:, x % G, :].bitcast(F32), ALU.subtract).then_inc(g_lo_done, 1)
                    if kind == "M2" and x == HT - 1:
                        dve.wait_ge(res_ready, t + 1)
                        for i in range(TT):
                            dve.wait_ge(acc_filled, t * TT + i + 1)
                            dve.tensor_tensor(res[:, i, :], psum[:, ACC + i, :], res[:, i, :],
                                              ALU.add).then_inc(acc_read, 1)

            dve.sem_inc(t_lo, 2)
            dve.sem_inc(g_lo_done, 2)
            dve.sem_inc(acc_read, TT)
            walk(dve, stages)

        @block.gpsimd
        def _(pool):
            pool.memset(ident[:, :], 0.0).then_inc(ident_zero, 1)
            pool.wait_ge(ident_zero, 1)
            pool.affine_select(out=ident[:, :], in_=ident[:, :], compare_op=ALU.not_equal, fill=1.0,
                               base=0, pattern=[[-1, P]], channel_multiplier=1).then_inc(ident_ready, 1)
            pool.wait_ge(const_loaded, 48)

            def stages(t, todo):
                for kind, x in todo:
                    if kind == "R":
                        for i in range(TT):
                            pool.wait_ge(res_loaded, t * 32 + 32)
                            inst = pool.tensor_tensor(res[:, i, :], res[:, i, :], b2_rows[:, :], ALU.add)
                            if i == TT - 1:
                                inst.then_inc(res_ready, 1)

            walk(pool, stages)

        @block.sync
        def _(sp):
            sp.dma_start(b1_col[:, :], b1).then_inc(const_loaded, 16)
            sp.dma_start(norm_col[:, :], norm_w).then_inc(const_loaded, 16)
            sp.dma_start(b2_rows[:, :], b2.to_broadcast((P, F))).then_inc(const_loaded, 16)
            w1_rows = w1.rearrange("(t p) n -> p t n", p=P)
            w2_rows = w2.rearrange("(t p) n -> p t n", p=P)

            def stages(t, todo):
                for kind, x in todo:
                    if kind == "W":
                        if x >= 2:
                            sp.wait_ge(w_lo, 2 * (x - 1))
                        sp.dma_start(stage1[:, x % 2, :, :], w1_rows[:, :, x * CHUNK:(x + 1) * CHUNK])\
                            .then_inc(w_loaded[x % 2], 16)
                        sp.dma_start(stage2[:, x % 2, :, :], w2_rows[:, 2 * x:2 * x + 2, :])\
                            .then_inc(w_loaded[x % 2], 16)
                    if kind == "L":
                        if x == 0:
                            wait_apart(sp, started, (t_filled, t * FT + FT))
                        for b in range(2):
                            sp.dma_start(xt[:, QT * b:QT * (b + 1), :],
                                         y_mid[(t + x + 1) * 2 + b].rearrange("(q p) n -> p q n", p=P))\
                                .then_inc(x_loaded, 16)
                    if kind == "R":
                        wait_apart(sp, started, (y_stored, t * 32 + 32))
                        for b in range(2):
                            sp.dma_start(res[:, QT * b:QT * (b + 1), :],
                                         latents[t * 2 + b].rearrange("(q p) n -> p q n", p=P))\
                                .then_inc(res_loaded, 16)
                    if kind == "M2" and x == HT - 1:
                        for b in range(2):
                            wait_apart(sp, started, (acc_read, t * TT + QT * (b + 1) + TT))
                            sp.dma_start(y_out[t * 2 + b].rearrange("(q p) n -> p q n", p=P),
                                         res[:, QT * b:QT * (b + 1), :]).then_inc(y_stored, 16)

            sp.sem_inc(started, 1)
            sp.sem_inc(y_stored, 32)
            walk(sp, stages)
            sp.wait_ge(y_stored, 32 * PAIRS + 32)


def attention1(nc, psum, query, context, w_q, w_k, w_v, w_out, b_out, y_out):
    B, C, L = query.shape
    CT = C // P
    KT = L // P
    D = 16
    HEADS = C // D
    ROWS = 32
    HPG = P // ROWS
    GROUPS = HEADS // HPG
    SCALE = D ** -0.5
    RING = 4
    TURN = 2 * GROUPS
    TURNS = B // 2
    HALVES = 2
    HKT = KT // HALVES
    NST = HALVES * HPG
    OPS = 96
    GEN = (4, 5, 6)
    OBANK = 7

    with ExitStack() as ctx:
        def sb(name, shape, dt=F32):
            return ctx.enter_context(nc.sbuf_tensor("a1_" + name, shape, dt))

        def sem(name):
            return ctx.enter_context(nc.semaphore("a1_" + name))

        W_hi = sb("W_hi", [P, 3, CT, C], F32R)
        W_lo = sb("W_lo", [P, 3, CT, C], F32R)
        Wo_hi = sb("Wo_hi", [P, GROUPS, C], F32R)
        Wo_lo = sb("Wo_lo", [P, GROUPS, C], F32R)
        QKS = sb("QKS", [P, RING, HPG, 2 * L], F32R)
        PT = sb("PT", [P, NST, HKT * L])
        V = sb("V", [P, 2, KT, HEADS, ROWS])
        stage = sb("stage", [P, 2, CT, L])
        X_hi = sb("X_hi", [P, 2, CT, L], F32R)
        X_lo = sb("X_lo", [P, 2, CT, L], F32R)
        res = sb("res", [P, CT, L])
        O = sb("O", [P, GROUPS, L])
        O_hi = sb("O_hi", [P, GROUPS, L], F32R)
        O_lo = sb("O_lo", [P, GROUPS, L], F32R)
        srcA = sb("srcA", [P, 2 * L], F32R)
        srcB = sb("srcB", [P, 2 * L], F32R)
        srcC = sb("srcC", [P, 2 * L], F32R)
        recips = sb("recips", [P, 2, L])
        flat = sb("flat", [P, 2 * HPG * L // P])
        mrow = sb("mrow", [HPG, L], F32R)
        mx = sb("mx", [P, KT, HPG])
        ident = sb("ident", [P, P])
        bo = sb("bo", [P, CT])
        sums_d = nc.dram_tensor("sums_rows", (2, HPG, L), F32, kind="Internal").ap()
        recips_d = nc.dram_tensor("recips_rows", (2, HPG, L), F32, kind="Internal").ap()

        with ExitStack() as c0:
            w_loaded = c0.enter_context(nc.semaphore("a1p_w_loaded"))
            w_hi_done = c0.enter_context(nc.semaphore("a1p_w_hi_done"))
            zeroed = c0.enter_context(nc.semaphore("a1p_zeroed"))
            stagew = PT[:, 0:3, 0:CT * C].rearrange("p m (t n) -> p m t n", t=CT)
            stageo = PT[:, 3, 0:GROUPS * C].rearrange("p (g n) -> p g n", g=GROUPS)
            block = c0.enter_context(nc.Block())

            @block.sync
            def _(sp):
                for m, w in enumerate((w_q, w_k, w_v)):
                    sp.dma_start(stagew[:, m, :, :], w.rearrange("(t p) n -> p t n", p=P))\
                        .then_inc(w_loaded, 16)
                sp.dma_start(stageo, w_out.rearrange("g p n -> p g n")).then_inc(w_loaded, 16)
                sp.dma_start(bo[:, :], b_out).then_inc(w_loaded, 16)
                sp.wait_ge(w_loaded, 80)

            @block.scalar
            def _(act):
                act.wait_ge(w_loaded, 80)
                for m in range(3):
                    act.activation(W_hi[:, m, :, :], stagew[:, m, :, :], ACT.Copy).then_inc(w_hi_done, 1)
                act.activation(Wo_hi[:, :, :], stageo, ACT.Copy).then_inc(w_hi_done, 1)

            @block.vector
            def _(dve):
                dve.memset(QKS[32:64, :, :, :].bitcast(F32), 0.0)
                dve.memset(QKS[64:96, :, :, :].bitcast(F32), 0.0)
                dve.memset(QKS[96:97, :, :, L:2 * L].bitcast(F32), 1.0)
                for m in range(3):
                    dve.wait_ge(w_hi_done, m + 1)
                    dve.tensor_tensor(W_lo[:, m, :, :], stagew[:, m, :, :],
                                      W_hi[:, m, :, :].bitcast(F32), ALU.subtract)
                dve.wait_ge(w_hi_done, 4)
                dve.tensor_tensor(Wo_lo[:, :, :], stageo, Wo_hi[:, :, :].bitcast(F32), ALU.subtract)

            @block.gpsimd
            def _(pool):
                pool.memset(V[:, :, :, :, :], 1.0)
                pool.memset(ident[:, :], 0.0).then_inc(zeroed, 1)
                pool.wait_ge(zeroed, 1)
                pool.affine_select(out=ident[:, :], in_=ident[:, :], compare_op=ALU.not_equal, fill=1.0,
                                   base=0, pattern=[[-1, P]], channel_multiplier=1)

        gen_filled = sem("gen_filled")
        gen_released = sem("gen_released")
        x_loaded = sem("x_loaded")
        x_hi = sem("x_hi")
        x_lo = sem("x_lo")
        qk_hi = sem("qk_hi")
        qk_copied = sem("qk_copied")
        stack_loaded = [sem(f"stack_loaded{r}") for r in range(RING)]
        max_loaded = sem("max_loaded")
        st_filled = sem("st_filled")
        exp_done = sem("exp_done")
        av_done = sem("av_done")
        o_copied = sem("o_copied")
        sums_stored = sem("sums_stored")
        sums_loaded = sem("sums_loaded")
        recip_done = sem("recip_done")
        recips_stored = sem("recips_stored")
        recips_loaded = sem("recips_loaded")
        o_scaled = sem("o_scaled")
        o_hi = sem("o_hi")
        o_lo = sem("o_lo")
        res_loaded = sem("res_loaded")
        y_stored = sem("y_stored")
        started = [sem("pool_started"), sem("sp_started")]
        STACK = 16 * 3 * HPG
        LAPS = TURN // RING

        USES = {"S": 2, "Q": 1, "K": 1, "M": 1, "V": 1, "OUT": 1}

        PROLOGUE = [("XL", 0, 0), ("X", 0, 0), ("Q", 0, 0), ("K", 0, 0)]
        PROLOGUE += [("V", 0, n) for n in range(KT)]
        PROLOGUE += [("S", 0, i) for i in range(NST)] + [("M", 0, 0)]

        def step(lu, first, last):
            g, b = lu % GROUPS, lu // GROUPS
            score = not (last and lu == TURN - 1)
            more = not (last and lu >= GROUPS)
            project = lu % 2 == 0 and not (last and lu == TURN - 2)
            before = not (first and lu == 0)
            out = [("XL", b + 1, 0)] * (g == 0 and more)
            for i in range(NST):
                out += [("ST", lu, i)] + [("S", lu + 1, i)] * score
                if i == 1:
                    out += [("Q", lu // 2 + 1, 0)] * project
                if i == 2:
                    out += [("K", lu // 2 + 1, 0)] * project
                if i == 3:
                    out += [("R", lu // 2 - 1, 0)] * (lu % 2 == 0 and before)
                    out += [("X", b + 1, 0)] * (g == 1 and more)
                if i == 5:
                    out += [("AV", lu, 0)]
            out += [("SC", lu // 2 - 1, 0)] * (lu % 2 == 0 and before)
            if g == 1 and not (first and b == 0):
                out += [("OUT", b - 1, 0), ("OUT", b - 1, 1)]
            if g >= 2 and more:
                out += [("V", b + 1, 2 * (g - 2)), ("V", b + 1, 2 * (g - 2) + 1)]
            if g == 3:
                out += [("RL", b, 0)]
            return out + [("M", lu + 1, 0)] * score + [("AV", lu, 1)]

        def counted(stages, n):
            out = []
            for stage in stages:
                out.append((*stage, n))
                n += USES.get(stage[0], 0)
            return out, n

        prologue, n0 = counted(PROLOGUE, 0)
        first_turn, n1 = counted([s for lu in range(TURN) for s in step(lu, True, False)], n0)
        PER_TURN = sum(USES.get(s[0], 0) for lu in range(TURN) for s in step(lu, False, False))
        assert PER_TURN % len(GEN) == 0
        turn, _ = counted([s for lu in range(TURN) for s in step(lu, False, False)], n1 - PER_TURN)
        last_turn, _ = counted([s for lu in range(TURN) for s in step(lu, False, True)]
                               + [("R", TURN // 2 - 1, 0), ("SC", TURN // 2 - 1, 0),
                                  ("OUT", 1, 0), ("OUT", 1, 1)], n1 - PER_TURN)

        def walk(eng, stage_of):
            stage_of(0, prologue + first_turn)
            with eng.Fori(1, TURNS - 1) as t:
                stage_of(t, turn)
            stage_of(TURNS - 1, last_turn)

        block = ctx.enter_context(nc.Block())

        @block.tensor
        def _(pe):
            def claim(t, n):
                if n >= len(GEN) or not isinstance(t, int) or t > 0:
                    pe.wait_ge(gen_released, t * PER_TURN + n - len(GEN) + 1)
                return GEN[n % len(GEN)]

            def stages(t, todo):
                for kind, v, x, n in todo:
                    if kind in ("Q", "K", "V") and x == 0:
                        b = v if kind == "V" else v // 2
                        pe.wait_ge(x_lo, t * 4 + 2 * (b + 1))
                    if kind in ("Q", "K"):
                        m = 0 if kind == "Q" else 1
                        cs = slice((v % 2) * P, (v % 2 + 1) * P)
                        bank = claim(t, n)
                        for ct in range(CT):
                            mm = split_product(pe, psum[:, bank, :], W_hi[:, m, ct, cs], W_lo[:, m, ct, cs],
                                               X_hi[:, m, ct, :], X_lo[:, m, ct, :], ct == 0, ct == CT - 1)
                        mm.then_inc(gen_filled, 1)
                    if kind == "V":
                        ks = slice(x * P, (x + 1) * P)
                        bank = claim(t, n)
                        for ct in range(CT):
                            mm = split_product(pe, psum[:, bank, 0:C], X_hi[:, 1, ct, ks], X_lo[:, 1, ct, ks],
                                               W_hi[:, 2, ct, :], W_lo[:, 2, ct, :], ct == 0, ct == CT - 1)
                        mm.then_inc(gen_filled, 1)
                    if kind == "S":
                        slot = v % RING
                        if x == 0:
                            pe.wait_ge(stack_loaded[slot], t * (LAPS * STACK) + (v // RING + 1) * STACK)
                        for k in range(2):
                            q = 2 * (x % 2) + k
                            bank = claim(t, n + k)
                            pe.matmul(psum[:, bank, :], QKS[0:OPS, slot, x // 2, q * P:(q + 1) * P],
                                      QKS[0:OPS, slot, x // 2, L:2 * L], start=True,
                                      stop=True).then_inc(gen_filled, 1)
                    if kind == "M":
                        last_s = max(m for k, u, _, m in todo if k == "S" and u == v) + 2
                        pe.wait_ge(gen_released, t * PER_TURN + last_s)
                        bank = claim(t, n)
                        for q in range(KT):
                            mm = pe.transpose(psum[0:HPG, bank, q * P:(q + 1) * P], mx[:, q, :],
                                              ident[:, :])
                        mm.then_inc(gen_filled, 1)
                    if kind == "ST":
                        slot, half, j, s = v % RING, x // HPG, x % HPG, NST * v + x
                        if x == 0:
                            pe.wait_ge(max_loaded, t * (16 * TURN) + 16 * (v + 1))
                        pe.wait_ge(exp_done, t * (TURN * NST) + s + 1)
                        for k in range(HKT):
                            kt = half * HKT + k
                            mm = pe.matmul(psum[:, (s % 2) * HKT + k, :],
                                           QKS[0:OPS + 1, slot, j, L + kt * P:L + (kt + 1) * P],
                                           QKS[0:OPS + 1, slot, j, 0:L], start=True, stop=True)
                        mm.then_inc(st_filled, 1)
                    if kind == "AV":
                        g, b = v % GROUPS, v // GROUPS
                        pe.wait_ge(exp_done, t * (TURN * NST) + NST * v + HPG * (x + 1) + 2)
                        if x == 0:
                            pe.wait_ge(o_copied, t * TURN + v + 1)
                        for k in range(HKT):
                            kt = x * HKT + k
                            for j in range(HPG):
                                mm = pe.matmul(psum[j * ROWS:(j + 1) * ROWS, OBANK, :],
                                               V[:, b % 2, kt, g * HPG + j, :],
                                               PT[:, x * HPG + j, k * L:(k + 1) * L],
                                               start=(kt == 0), stop=(kt == KT - 1), skip_group_check=True)
                        mm.then_inc(av_done, 1)
                    if kind == "OUT":
                        if x == 0:
                            pe.wait_ge(o_lo, t * TURN + GROUPS * (v + 1) + GROUPS)
                        cs = slice(x * P, (x + 1) * P)
                        bank = claim(t, n)
                        for g in range(GROUPS):
                            mm = split_product(pe, psum[:, bank, :], Wo_hi[:, g, cs], Wo_lo[:, g, cs],
                                               O_hi[:, g, :], O_lo[:, g, :], g == 0, g == GROUPS - 1)
                        mm.then_inc(gen_filled, 1)

            pe.sem_inc(av_done, 2)
            walk(pe, stages)

        @block.scalar
        def _(act):
            def stages(t, todo):
                for kind, v, x, n in todo:
                    if kind == "X":
                        act.wait_ge(x_loaded, t * 64 + 32 * (v + 1))
                        for m in range(2):
                            act.activation(X_hi[:, m, :, :], stage[:, m, :, :], ACT.Copy).then_inc(x_hi, 1)
                    if kind in ("Q", "K"):
                        act.wait_ge(gen_filled, t * PER_TURN + n + 1)
                        if kind == "Q" and v > 0:
                            for u in (2 * v - 2, 2 * v - 1):
                                act.wait_ge(stack_loaded[u % RING], t * (LAPS * STACK)
                                            + (u // RING + 1) * STACK)
                        cols = slice(0, L) if kind == "Q" else slice(L, 2 * L)
                        act.activation(srcA[:, cols], psum[:, GEN[n % len(GEN)], :],
                                       ACT.Copy).then_inc(qk_hi, 1)
                    if kind == "ST":
                        s = NST * v + x
                        act.wait_ge(st_filled, t * (TURN * NST) + s + 1)
                        if x % HPG == 0:
                            act.wait_ge(av_done, t * (2 * TURN) + 2 * v + x // HPG + 1)
                        act.activation(PT[:, x, :],
                                       psum[:, (s % 2) * HKT:(s % 2 + 1) * HKT, :]
                                       .rearrange("p s n -> p (s n)"),
                                       ACT.Exp, scale=SCALE).then_inc(exp_done, 1)
                    if kind == "AV" and x == 1:
                        act.wait_ge(av_done, t * (2 * TURN) + 2 * v + 2 + 2)
                        act.wait_ge(o_lo, t * TURN + v + 1)
                        act.activation(O[:, v % GROUPS, :], psum[:, OBANK, :],
                                       ACT.Copy).then_inc(o_copied, 1)
                    if kind == "SC":
                        for u in (2 * v, 2 * v + 1):
                            act.wait_ge(o_scaled, t * TURN + u + 1)
                            act.activation(O_hi[:, u % GROUPS, :], O[:, u % GROUPS, :],
                                           ACT.Copy).then_inc(o_hi, 1)

            act.sem_inc(exp_done, 2)
            act.sem_inc(o_copied, 1)
            walk(act, stages)

        @block.vector
        def _(dve):
            def stages(t, todo):
                for kind, v, x, n in todo:
                    bank = GEN[n % len(GEN)]
                    if kind == "X":
                        for m in range(2):
                            dve.wait_ge(x_hi, t * 4 + 2 * v + m + 1)
                            dve.tensor_tensor(X_lo[:, m, :, :], stage[:, m, :, :],
                                              X_hi[:, m, :, :].bitcast(F32), ALU.subtract).then_inc(x_lo, 1)
                    if kind in ("Q", "K"):
                        dve.wait_ge(qk_hi, t * TURN + 2 * v + (1 if kind == "Q" else 2))
                        cols, lo = (slice(0, L), srcC) if kind == "Q" else (slice(L, 2 * L), srcB)
                        dve.tensor_tensor(lo[:, cols], psum[:, bank, :], srcA[:, cols].bitcast(F32),
                                          ALU.subtract).then_inc(gen_released, 1)
                    if kind == "V":
                        dve.wait_ge(gen_filled, t * PER_TURN + n + 1)
                        dve.tensor_copy(V[:, v % 2, x, :, 0:D],
                                        psum[:, bank, 0:C].rearrange("p (h d) -> p h d", d=D))\
                            .then_inc(gen_released, 1)
                    if kind == "S":
                        for k in range(2):
                            q = 2 * (x % 2) + k
                            dve.wait_ge(gen_filled, t * PER_TURN + n + k + 1)
                            dve.tensor_reduce(mx[:, q, x // 2:x // 2 + 1], psum[:, GEN[(n + k) % len(GEN)], :],
                                              AX_X, ALU.max).then_inc(gen_released, 1)
                    if kind == "M":
                        dve.wait_ge(gen_filled, t * PER_TURN + n + 1)
                        if v > 0:
                            dve.wait_ge(max_loaded, t * (16 * TURN) + 16 * v)
                        dve.tensor_scalar(mrow[:, :], psum[0:HPG, bank, :], -1.0, None,
                                          ALU.mult).then_inc(gen_released, 1)
                    if kind == "SC":
                        dve.wait_ge(sums_loaded, t * (16 * TURN // 2) + 16 * (v + 1))
                        dve.reciprocal(flat[:, :], flat[:, :]).then_inc(recip_done, 1)
                    if kind == "OUT":
                        if x == 0:
                            dve.wait_ge(res_loaded, t * 32 + 16 * (v + 1))
                        dve.wait_ge(gen_filled, t * PER_TURN + n + 1)
                        dve.scalar_tensor_tensor(out=res[:, x, :], in0=psum[:, bank, :],
                                                 scalar=bo[:, x:x + 1], in1=res[:, x, :], op0=ALU.add,
                                                 op1=ALU.add).then_inc(gen_released, 1)

            dve.wait_ge(x_loaded, 32)
            walk(dve, stages)

        @block.gpsimd
        def _(pool):
            def stages(t, todo):
                for kind, v, x, n in todo:
                    if kind in ("Q", "K"):
                        wait_apart(pool, started[0],
                                   (qk_hi, t * TURN + 2 * v + (1 if kind == "Q" else 2)))
                        cols, copy = (slice(0, L), srcB) if kind == "Q" else (slice(L, 2 * L), srcC)
                        pool.tensor_copy(copy[:, cols], srcA[:, cols]).then_inc(qk_copied, 1)
                    if kind == "AV" and x == 1:
                        waits = [(o_copied, t * TURN + v + 1 + 1)]
                        if v >= 2:
                            waits.append((sums_loaded, t * (16 * TURN // 2) + 16 * (v // 2)))
                        wait_apart(pool, started[0], *waits)
                        pool.dma_start(sums_d[v % 2], O[D:P:ROWS, v % GROUPS, :]).then_inc(sums_stored, 16)
                    if kind == "R":
                        wait_apart(pool, started[0], (sums_stored, t * (16 * TURN) + 32 * (v + 1)))
                        pool.dma_start(flat[:, :], sums_d.rearrange("u j (c n) -> (u j c) n", n=flat.shape[1]))\
                            .then_inc(sums_loaded, 16)
                    if kind == "SC":
                        wait_apart(pool, started[0], (recip_done, t * (TURN // 2) + v + 1))
                        pool.dma_start(recips_d.rearrange("u j (c n) -> (u j c) n", n=flat.shape[1]),
                                       flat[:, :]).then_inc(recips_stored, 16)
                        wait_apart(pool, started[0], (recips_stored, t * (16 * TURN // 2) + 16 * (v + 1)))
                        for j in range(HPG):
                            pool.dma_start(recips[j * ROWS:(j + 1) * ROWS, :, :],
                                           recips_d[:, j:j + 1, :].rearrange("u j n -> j u n")
                                           .to_broadcast((ROWS, 2, L))).then_inc(recips_loaded, 16)
                        for k in range(2):
                            u = (2 * v + k) % GROUPS
                            pool.wait_ge(recips_loaded, t * (64 * TURN // 2) + 64 * (v + 1))
                            pool.tensor_tensor(O[:, u, :], O[:, u, :], recips[:, k, :],
                                               ALU.mult).then_inc(o_scaled, 1)
                        for k in range(2):
                            u = (2 * v + k) % GROUPS
                            pool.wait_ge(o_hi, t * TURN + 2 * v + k + 1)
                            pool.tensor_tensor(O_lo[:, u, :], O[:, u, :], O_hi[:, u, :].bitcast(F32),
                                               ALU.subtract).then_inc(o_lo, 1)

            pool.sem_inc(started[0], 1)
            pool.sem_inc(o_lo, GROUPS)
            walk(pool, stages)

        @block.sync
        def _(sp):
            def stages(t, todo):
                for kind, v, x, n in todo:
                    if kind == "XL":
                        if not (isinstance(t, int) and t * 2 + v == 0):
                            wait_apart(sp, started[1], (x_lo, t * 4 + 2 * v))
                        for m, src in enumerate((query, context)):
                            sp.dma_start(stage[:, m, :, :], src[t * 2 + v].rearrange("(c p) n -> p c n", p=P))\
                                .then_inc(x_loaded, 16)
                    if kind == "K":
                        wait_apart(sp, started[1], (qk_copied, t * TURN + 2 * (v + 1)),
                                   (gen_released, t * PER_TURN + n + 1))
                        for w in range(2):
                            u = 2 * v + w
                            if not isinstance(t, int) or t * TURN + u >= RING:
                                wait_apart(sp, started[1],
                                           (st_filled, t * (TURN * NST) + NST * (u - RING + 1)))
                            for j in range(HPG):
                                rows = slice((w * HPG + j) * D, (w * HPG + j + 1) * D)
                                for r, src in enumerate((srcA, srcB, srcC)):
                                    sp.dma_start(QKS[r * D:(r + 1) * D, u % RING, j, :].bitcast(F32),
                                                 src[rows, :].bitcast(F32)).then_inc(stack_loaded[u % RING], 16)
                    if kind == "M":
                        sp.wait_ge(gen_released, t * PER_TURN + n + 1)
                        sp.dma_start(QKS[OPS:OPS + 1, v % RING, :, 0:L].bitcast(F32),
                                     mrow[:, :].bitcast(F32)).then_inc(max_loaded, 16)
                    if kind == "RL":
                        wait_apart(sp, started[1], (y_stored, t * 32 + 16 * v + 16))
                        sp.dma_start(res[:, :, :], query[t * 2 + v].rearrange("(c p) n -> p c n", p=P))\
                            .then_inc(res_loaded, 16)
                    if kind == "OUT" and x == 1:
                        wait_apart(sp, started[1], (gen_released, t * PER_TURN + n + 1))
                        sp.dma_start(y_out[t * 2 + v].rearrange("(c p) n -> p c n", p=P), res[:, :, :])\
                            .then_inc(y_stored, 16)

            sp.sem_inc(started[1], 1)
            sp.sem_inc(y_stored, 16)
            walk(sp, stages)
            sp.wait_ge(y_stored, 16 * B + 16)


def arrays(inputs):
    import numpy as np
    a = {n: np.asarray(v) for n, v in inputs.items()}
    ctx, x = a["ctx_2048"], a["x"]
    kv = a["L0_xattn_kv_w"].reshape(512, 512, 2)
    kvb = a["L0_xattn_kv_b"].reshape(512, 2)
    b_qkv = np.stack([a["L0_xattn_q_b"], kvb[:, 0], kvb[:, 1]]).reshape(3, 4, 128).transpose(2, 0, 1)
    out = {
        "latents": x, "ctx": ctx, "mask": a["mask_BxS2_ik0"],
        "hT": np.concatenate([ctx.transpose(0, 2, 1), x.transpose(0, 2, 1)], axis=2),
        "wq0": a["L0_xattn_q_w"], "wk0": kv[:, :, 0], "wv0": kv[:, :, 1], "wo0": a["L0_xattn_out_w"],
        "b_qkv": b_qkv, "b_out": a["L0_xattn_out_b"].reshape(1, 512),
        "norm_w": a["L0_xattn_postnorm_w"].reshape(4, 128).T,
        "w1": a["L0_xattn_mlp_w1"], "b1": a["L0_xattn_mlp_b1"].reshape(16, 128).T,
        "w2": a["L0_xattn_mlp_w2"], "b2": a["L0_xattn_mlp_b2"].reshape(1, 512),
    }
    for m in "qkv":
        out["w%s1" % m] = a["L1_xattn_W" + m].T
    wo = np.zeros((4, 4, 32, 256), np.float32)
    wo[:, :, 0:16] = a["L1_xattn_Wo"].T.reshape(4, 4, 16, 256)
    out["wo1"] = wo.reshape(4, 128, 256)
    out["bo1"] = a["L1_xattn_bo"].reshape(2, 128).T
    return {n: np.ascontiguousarray(v) for n, v in out.items()}


def program(nc, aps):
    shape = tuple(aps["latents"].shape)
    y = nc.dram_tensor("y", shape, F32, kind="ExternalOutput").ap()
    y_mid = nc.dram_tensor("y_mid", shape, F32, kind="Internal").ap()
    y_mlp = nc.dram_tensor("y_mlp", shape, F32, kind="Internal").ap()
    with nc.psum_tensor("ps", [P, 8, BANK], F32) as psum:
        attention0(nc, psum, aps["latents"], aps["hT"], aps["mask"], aps["wq0"], aps["wk0"], aps["wv0"],
                   aps["wo0"], aps["b_qkv"], aps["b_out"], y_mid)
        mlp(nc, psum, y_mid, aps["latents"], aps["w1"], aps["w2"], aps["b1"], aps["b2"], aps["norm_w"],
            y_mlp)
        attention1(nc, psum, y_mlp, aps["ctx"], aps["wq1"], aps["wk1"], aps["wv1"], aps["wo1"],
                   aps["bo1"], y)


def kernel(**inputs):
    import concourse.bacc as bacc
    from concourse.bass_utils import run_bass_kernel_spmd

    nc = bacc.Bacc("TRN2", target_bir_lowering=False, num_devices=1)
    arr = arrays(inputs)
    aps = {name: nc.dram_tensor(name, v.shape, mybir.dt.from_np(v.dtype), kind="ExternalInput").ap()
           for name, v in arr.items()}
    program(nc, aps)
    return run_bass_kernel_spmd(nc, [arr], core_ids=[0]).results[0]["y"]
```

```python
from contextlib import ExitStack

import concourse.bass as bass
from concourse import mybir

F32 = mybir.dt.float32
F32R = mybir.dt.float32r
I32 = mybir.dt.int32
ALU = mybir.AluOpType
ACT = mybir.ActivationFunctionType
AX_X = mybir.AxisListType.X

P = 128
BANK = 512
MASKED = -1.0e30


def split_product(pe, out, w_hi, w_lo, m_hi, m_lo, first, last):
    pe.matmul(out, w_hi, m_hi, start=first, stop=False)
    pe.matmul(out, w_hi, m_lo, start=False, stop=False)
    return pe.matmul(out, w_lo, m_hi, start=False, stop=last)


def wait_apart(eng, started, *waits):
    values = [value if isinstance(value, int) else eng.to_reg(value) for _, value in waits]
    eng.wait_ge(started, 1)
    for (sem, _), value in zip(waits, values):
        eng.wait_ge(sem, value)


def attention0(nc, psum, latents, hT, mask, w_q, w_k, w_v, w_out, b_qkv, b_out, y_mid):
    B, LAT, F = latents.shape
    KEYS = hT.shape[2]
    FT = F // P
    KT = KEYS // P
    QT = LAT // P
    D = 32
    HPG = P // D
    UNITS = B * FT
    SCALE = 1.0 / D
    RING = 4
    AHEAD = 3
    TURN = 2 * FT
    TURNS = B // 2
    QK = LAT + KEYS
    HALVES = KT * LAT // BANK
    PIECES = HPG * HALVES
    ST_BANKS = 3
    GEN = (3, 4, 5, 6)
    OBANK = 7
    PT_HEADS = 2 * HPG

    with ExitStack() as ctx:
        def sb(name, shape, dt=F32):
            return ctx.enter_context(nc.sbuf_tensor("a0_" + name, shape, dt))

        def sem(name):
            return ctx.enter_context(nc.semaphore("a0_" + name))

        W_hi = sb("W_hi", [P, 4, FT, F], F32R)
        W_lo = sb("W_lo", [P, 4, FT, F], F32R)
        QKS = sb("QKS", [P, RING, HPG, QK], F32R)
        PT = sb("PT", [P, PT_HEADS, KT * LAT])
        V = sb("V", [P, 2, KT, F])
        hT_hi = sb("hT_hi", [P, FT, KEYS], F32R)
        hT_lo = sb("hT_lo", [P, FT, KEYS], F32R)
        stage = sb("stage", [P, 2, KEYS])
        OT_hi = sb("OT_hi", [P, FT, LAT], F32R)
        OT_lo = sb("OT_lo", [P, FT, LAT], F32R)
        srcA = sb("srcA", [P, QK], F32R)
        srcB = sb("srcB", [P, QK], F32R)
        srcC = sb("srcC", [P, QK], F32R)
        xb = sb("xb", [P, QT, F])
        bo = sb("bo", [P, F])
        ident = sb("ident", [P, P])
        ones = sb("ones", [P, D])
        bias = sb("bias", [P, 3, FT])
        rsum = sb("rsum", [P, LAT])
        oscaled = sb("oscaled", [P, LAT])
        mx = sb("mx", [P, QT, HPG])
        mrow = sb("mrow", [HPG, LAT], F32R)
        mask_d = nc.dram_tensor("mask_rows", (B, 1, HPG, KEYS), F32, kind="Internal").ap()

        mask_i = xb[0:B, 0, 0:KEYS - LAT].bitcast(I32)
        mask_r = bo[0:B, :]
        stagew = PT[:, :, :].rearrange("p (m s) n -> p m (s n)", m=4)

        w_loaded = [sem(f"w_loaded{m}") for m in range(4)]
        small_loaded = sem("small_loaded")
        bo_loaded = sem("bo_loaded")
        w_hi = sem("w_hi")
        w_lo = sem("w_lo")
        masked = sem("masked")
        mask_stored = sem("mask_stored")
        ident_zero = sem("ident_zero")
        ident_ready = sem("ident_ready")
        ones_ready = sem("ones_ready")
        fixed_rows = sem("fixed_rows")
        gen_filled = sem("gen_filled")
        gen_released = sem("gen_released")
        ht_loaded = [sem("ht_loaded0"), sem("ht_loaded1")]
        ht_hi = sem("ht_hi")
        ht_lo = sem("ht_lo")
        qk_hi = sem("qk_hi")
        qk_copied = sem("qk_copied")
        stack_loaded = [sem(f"stack_loaded{r}") for r in range(RING)]
        max_loaded = sem("max_loaded")
        st_filled = sem("st_filled")
        exp_done = sem("exp_done")
        av_done = sem("av_done")
        outs_done = sem("outs_done")
        half_added = sem("half_added")
        half_added_pool = sem("half_added_pool")
        added = sem("added")
        added_pool = sem("added_pool")
        recip_done = sem("recip_done")
        o_scaled = sem("o_scaled")
        o_hi = sem("o_hi")
        o_lo = sem("o_lo")
        x_loaded = [sem(f"x_loaded{t}") for t in range(QT)]
        bo_added = sem("bo_added")
        y_stored = [sem(f"y_stored{t}") for t in range(QT)]
        mask_loaded = [sem(f"mask_loaded{r}") for r in range(RING)]
        STACK = 16 * 3 * HPG

        PROLOGUE = [("HL", 0, 0), ("HL", 0, 1), ("HT", 0, 0), ("HL", 0, 2), ("HT", 0, 1), ("HL", 0, 3),
                    ("HT", 0, 2), ("HT", 0, 3), ("Q", 0, 0), ("K", 0, 0), ("STACK", 0, 0),
                    ("HL", 1, 0), ("HL", 1, 1), ("Q", 1, 0), ("K", 1, 0), ("V", 0, 0), ("V", 0, 1)]
        PROLOGUE += [("S", 0, j) for j in range(HPG)] + [("M", 0, 0), ("STACK", 1, 0)]
        PROLOGUE += [("Q", 2, 0), ("K", 2, 0), ("V", 0, 2), ("V", 0, 3), ("S", 1, 0), ("STACK", 2, 0)]

        def step(lu, first, last):
            g, b = lu % FT, lu // FT
            units = TURN if last else 2 * TURN
            project = lu + AHEAD < units
            more = not (last and b == 1)
            out = []
            for j in range(HPG):
                out += [("ST", lu, j)]
                if not (first and lu == 0):
                    out += [("AV", lu - 1, x) for x in ((0,), (1,), (), (2,))[j]]
                if j < 2 and g == 1 and not (first and b == 0):
                    out += [("OUT", b - 1, j)]
                if j == 3 and lu + 1 < units:
                    out += [("M", lu + 1, 0)]
                if j == 3 and g == 0 and more:
                    out += [("HT", b + 1, 0), ("HT", b + 1, 1), ("HL", b + 1, 2), ("HL", b + 1, 3)]
                u, part = lu + 1 + (j + 1) // HPG, (j + 1) % HPG
                if u < units:
                    out += [("S", u, part)]
                out += [("ADD", lu - 1, 0)] * (j == 1 and not (first and lu == 0))
                out += [("Q", lu + AHEAD, 0)] * (j == 1 and project)
                out += [("K", lu + AHEAD, 0)] * (j == 2 and project)
            out += [("N", lu - 1, 0)] * (not (first and lu == 0))
            out += [("STACK", lu + AHEAD, 0)] * project
            if g == 0:
                out += [("HT", b + 1, 2), ("HT", b + 1, 3)] * more
            out += [("V", b + 1, n) for n in ((), (0,), (1, 2), (3,))[g]] * more
            if g == 1:
                out += [("HL", b + 2, 0), ("HL", b + 2, 1)] * (not last)
            if g == 2:
                out += [("XL", b, 0), ("XL", b, 1)]
            if g == 3:
                out += [("XB", b, 0), ("XB", b, 1)]
            return out

        USES = {"S": QT, "Q": 1, "K": 1, "M": 1, "V": 1, "OUT": 1}

        def counted(stages, n):
            out = []
            for stage in stages:
                out.append((*stage, n))
                n += USES.get(stage[0], 0)
            return out, n

        prologue, n0 = counted(PROLOGUE, 0)
        first_turn, n1 = counted([s for lu in range(TURN) for s in step(lu, True, False)], n0)
        PER_TURN = sum(USES.get(s[0], 0) for lu in range(TURN) for s in step(lu, False, False))
        assert PER_TURN % len(GEN) == 0
        N0 = n1 - PER_TURN
        turn, _ = counted([s for lu in range(TURN) for s in step(lu, False, False)], N0)
        last_turn, _ = counted([s for lu in range(TURN) for s in step(lu, False, True)]
                               + [("AV", TURN - 1, 0), ("AV", TURN - 1, 1), ("ADD", TURN - 1, 0),
                                  ("AV", TURN - 1, 2)] + [("N", TURN - 1, 0)]
                               + [("OUT", 1, 0), ("OUT", 1, 1)], N0)

        def walk(eng, stage_of, before=prologue):
            stage_of(0, before + first_turn)
            with eng.Fori(1, TURNS - 1) as t:
                stage_of(t, turn)
            stage_of(TURNS - 1, last_turn)

        started = [sem("pool_started"), sem("sp_started")]

        block = ctx.enter_context(nc.Block())

        def load_stack(eng, u, heads):
            for j in heads:
                rows = slice(j * D, (j + 1) * D)
                for r, src in enumerate((srcA, srcB, srcC)):
                    eng.dma_start(QKS[r * D:(r + 1) * D, u % RING, j, :].bitcast(F32),
                                  src[rows, :].bitcast(F32)).then_inc(stack_loaded[u % RING], 16)

        def add_up(eng, t, lv, heads, half, done):
            first = t * (2 * TURN) + 2 * lv
            for step_sem, before, n in ((half, None, 2 * LAT), (done, half, LAT)):
                for k, j in enumerate(heads):
                    head = (HPG * lv + j) % PT_HEADS
                    if before is not None:
                        eng.wait_ge(before, first + k + 1)
                    eng.tensor_tensor(PT[:, head, 0:n], PT[:, head, 0:n], PT[:, head, n:2 * n],
                                      ALU.add).then_inc(step_sem, 1)

        def staged(m):
            return stagew[:, m, :].rearrange("p (t n) -> p t n", t=FT)

        REST = prologue[prologue.index(("Q", 0, 0, 0)):]

        def start_up(stages, wait_and_split):
            wait_and_split(0)
            stages(0, prologue[2:5])
            wait_and_split(1)
            stages(0, prologue[5:8])
            stages(0, REST[0:2])

        @block.tensor
        def _(pe):
            def claim(t, n):
                if n >= len(GEN) or not (isinstance(t, int) and t == 0):
                    pe.wait_ge(gen_released, t * PER_TURN + n - len(GEN) + 1)
                return GEN[n % len(GEN)]

            def stages(t, todo):
                first_s = {}
                for kind, lv, x, n in todo:
                    slot, g, b = lv % RING, lv % FT, lv // FT
                    if kind in ("Q", "K", "V") and (kind != "V" or x == 0):
                        bb = b if kind != "V" else lv
                        pe.wait_ge(ht_lo, t * (2 * FT) + FT * (bb + 1))
                    if isinstance(t, int) and t == 0 and lv == 0 and x == 0 and kind in ("Q", "K", "V"):
                        pe.wait_ge(w_lo, "QKV".index(kind) + 1)
                    if kind in ("Q", "K"):
                        m, cols = (0, slice(KEYS - LAT, KEYS)) if kind == "Q" else (1, slice(0, KEYS))
                        bank = claim(t, n)
                        for ft in range(FT):
                            fs = slice(g * P, (g + 1) * P)
                            mm = split_product(pe, psum[:, bank, 0:cols.stop - cols.start],
                                               W_hi[:, m, ft, fs], W_lo[:, m, ft, fs],
                                               hT_hi[:, ft, cols], hT_lo[:, ft, cols],
                                               ft == 0, ft == FT - 1)
                        mm.then_inc(gen_filled, 1)
                    if kind == "V":
                        bank = claim(t, n)
                        for ft in range(FT):
                            ks = slice(x * P, (x + 1) * P)
                            mm = split_product(pe, psum[:, bank, :], hT_hi[:, ft, ks], hT_lo[:, ft, ks],
                                               W_hi[:, 2, ft, :], W_lo[:, 2, ft, :],
                                               ft == 0, ft == FT - 1)
                        mm.then_inc(gen_filled, 1)
                    if kind == "S":
                        if x == 0:
                            if isinstance(t, int) and t == 0 and lv < RING:
                                pe.wait_ge(fixed_rows, lv + 1)
                            pe.wait_ge(stack_loaded[slot], t * (TURN // RING * STACK)
                                       + (lv // RING + 1) * STACK)
                            pe.wait_ge(mask_loaded[slot], t * (TURN // RING * 16) + (lv // RING + 1) * 16)
                        for q in range(QT):
                            bank = claim(t, n + q)
                            pe.matmul(psum[:, bank, :], QKS[0:97, slot, x, q * P:(q + 1) * P],
                                      QKS[0:97, slot, x, LAT:QK], start=True,
                                      stop=True).then_inc(gen_filled, 1)
                    if kind == "M":
                        last_s = max(m for k, v, _, m in todo if k == "S" and v == lv) + QT
                        pe.wait_ge(gen_released, t * PER_TURN + last_s)
                        if isinstance(t, int) and t * TURN + lv == 0:
                            pe.wait_ge(ident_ready, 1)
                        bank = claim(t, n)
                        for q in range(QT):
                            mm = pe.transpose(psum[0:HPG, bank, q * P:(q + 1) * P], mx[:, q, :],
                                              ident[:, :])
                        mm.then_inc(gen_filled, 1)
                    if kind == "ST":
                        if x == 0:
                            pe.wait_ge(max_loaded, t * (16 * TURN) + 16 * (lv + 1))
                        for half in range(HALVES):
                            p = PIECES * lv + HALVES * x + half
                            if not (isinstance(t, int) and t == 0):
                                pe.wait_ge(exp_done, t * (TURN * PIECES) + max(0, p - ST_BANKS + 1))
                            elif p >= ST_BANKS:
                                pe.wait_ge(exp_done, p - ST_BANKS + 1)
                            for k in range(KT // HALVES):
                                kt = half * (KT // HALVES) + k
                                mm = pe.matmul(psum[:, p % ST_BANKS, k * LAT:(k + 1) * LAT],
                                               QKS[0:98, slot, x, LAT + kt * P:LAT + (kt + 1) * P],
                                               QKS[0:98, slot, x, 0:LAT], start=True, stop=True)
                            mm.then_inc(st_filled, 1)
                    if kind == "AV":
                        if x == 0:
                            pe.wait_ge(exp_done, t * (TURN * PIECES) + PIECES * (lv + 1))
                            pe.wait_ge(o_scaled, t * TURN + lv + 1)
                            if isinstance(t, int) and t * TURN + lv == 0:
                                pe.wait_ge(ones_ready, 1)
                        if x == 2:
                            pe.wait_ge(added, t * (2 * TURN) + 2 * (lv + 1))
                            pe.wait_ge(added_pool, t * (2 * TURN) + 2 * (lv + 1))
                        for kt in ((0, 1), (2, 3), (0,))[x]:
                            for j in range(HPG):
                                rows = slice(j * D, (j + 1) * D)
                                pt = PT[:, (HPG * lv + j) % PT_HEADS, kt * LAT:(kt + 1) * LAT]
                                f0 = g * P + j * D
                                if x < 2:
                                    mm = pe.matmul(psum[rows, OBANK, 0:LAT], V[:, b % 2, kt, f0:f0 + D], pt,
                                                   start=(kt == 0), stop=(kt == KT - 1),
                                                   skip_group_check=True)
                                else:
                                    mm = pe.matmul(psum[rows, OBANK, LAT:2 * LAT], ones[:, :], pt,
                                                   start=False, stop=True, skip_group_check=True)
                        if x == 1:
                            mm.then_inc(outs_done, 1)
                        if x == 2:
                            mm.then_inc(av_done, 1)
                    if kind == "OUT":
                        if x == 0:
                            pe.wait_ge(o_lo, t * TURN + FT * (lv + 1) + 1)
                            if isinstance(t, int) and t == 0 and lv == 0:
                                pe.wait_ge(w_lo, 4)
                        bank = claim(t, n)
                        for ft in range(FT):
                            ls = slice(x * P, (x + 1) * P)
                            mm = split_product(pe, psum[:, bank, :], OT_hi[:, ft, ls], OT_lo[:, ft, ls],
                                               W_hi[:, 3, ft, :], W_lo[:, 3, ft, :],
                                               ft == 0, ft == FT - 1)
                        mm.then_inc(gen_filled, 1)

            pe.sem_inc(av_done, 2)
            walk(pe, stages)

        @block.scalar
        def _(act):
            def stages(t, todo):
                for kind, lv, x, n in todo:
                    slot, g = lv % RING, lv % FT
                    if kind == "HT":
                        act.wait_ge(ht_loaded[x % 2], t * (16 * FT) + 16 * (FT // 2 * lv + x // 2 + 1))
                        act.activation(hT_hi[:, x, :], stage[:, x % 2, :], ACT.Copy).then_inc(ht_hi, 1)
                    if kind in ("Q", "K"):
                        act.wait_ge(gen_filled, t * PER_TURN + n + 1)
                        if kind == "Q" and not (isinstance(t, int) and t * TURN + lv == 0):
                            act.wait_ge(stack_loaded[(lv - 1) % RING], t * (TURN // RING * STACK)
                                        + ((lv - 1) // RING + 1) * STACK)
                        m, cols = (0, slice(0, LAT)) if kind == "Q" else (1, slice(LAT, QK))
                        act.activation(srcA[:, cols], psum[:, GEN[n % len(GEN)], 0:cols.stop - cols.start],
                                       ACT.Identity, bias=bias[:, m, g:g + 1]).then_inc(qk_hi, 1)
                    if kind == "ST":
                        h = HPG * lv + x
                        if isinstance(t, int) and t == 0 and h == 0:
                            act.wait_ge(w_lo, 4)
                        for half in range(HALVES):
                            p = PIECES * lv + HALVES * x + half
                            act.wait_ge(st_filled, t * (TURN * PIECES) + p + 1)
                            if x == 0 and half == 0:
                                act.wait_ge(av_done, t * TURN + lv + 1)
                            act.activation(PT[:, h % PT_HEADS, half * BANK:(half + 1) * BANK],
                                           psum[:, p % ST_BANKS, :], ACT.Exp,
                                           scale=SCALE).then_inc(exp_done, 1)
                    if kind == "N":
                        act.wait_ge(o_scaled, t * TURN + lv + 1 + 1)
                        act.activation(OT_hi[:, g, :], oscaled[:, :], ACT.Identity,
                                       bias=bias[:, 2, g:g + 1]).then_inc(o_hi, 1)

            def split_hi(m):
                act.wait_ge(w_loaded[m], 16)
                act.activation(W_hi[:, m, :, :], staged(m), ACT.Copy).then_inc(w_hi, 1)

            start_up(stages, split_hi)
            split_hi(2)
            act.wait_ge(qk_copied, 2)
            act.wait_ge(gen_released, 2)
            load_stack(act, 0, (2, 3))
            split_hi(3)
            walk(act, stages, REST[2:])

        @block.vector
        def _(dve):
            def stages(t, todo):
                for kind, lv, x, n in todo:
                    g = lv % FT
                    bank = GEN[n % len(GEN)]
                    if kind == "HT":
                        dve.wait_ge(ht_hi, t * (2 * FT) + FT * lv + x + 1)
                        dve.tensor_tensor(hT_lo[:, x, :], stage[:, x % 2, :], hT_hi[:, x, :].bitcast(F32),
                                          ALU.subtract).then_inc(ht_lo, 1)
                    if kind in ("Q", "K"):
                        dve.wait_ge(qk_hi, t * (2 * TURN) + 2 * lv + (1 if kind == "Q" else 2))
                        m, cols, lo = (0, slice(0, LAT), srcC) if kind == "Q" else (1, slice(LAT, QK), srcB)
                        dve.scalar_tensor_tensor(out=lo[:, cols], in0=psum[:, bank, 0:cols.stop - cols.start],
                                                 scalar=bias[:, m, g:g + 1], in1=srcA[:, cols].bitcast(F32),
                                                 op0=ALU.add, op1=ALU.subtract).then_inc(gen_released, 1)
                    if kind == "V":
                        dve.wait_ge(gen_filled, t * PER_TURN + n + 1)
                        dve.tensor_copy(V[:, lv % 2, x, :], psum[:, bank, :]).then_inc(gen_released, 1)
                    if kind == "S":
                        for q in range(QT):
                            dve.wait_ge(gen_filled, t * PER_TURN + n + q + 1)
                            dve.tensor_reduce(mx[:, q, x:x + 1], psum[:, GEN[(n + q) % len(GEN)], :], AX_X,
                                              ALU.max).then_inc(gen_released, 1)
                    if kind == "M":
                        dve.wait_ge(gen_filled, t * PER_TURN + n + 1)
                        if not (isinstance(t, int) and t * TURN + lv == 0):
                            dve.wait_ge(max_loaded, t * (16 * TURN) + 16 * lv)
                        dve.tensor_scalar(mrow[:, :], psum[0:HPG, bank, 0:LAT], -1.0, None,
                                          ALU.mult).then_inc(gen_released, 1)
                    if kind == "ADD":
                        dve.wait_ge(outs_done, t * TURN + lv + 1)
                        add_up(dve, t, lv, (0, 1), half_added, added)
                    if kind == "N":
                        dve.wait_ge(av_done, t * TURN + lv + 1 + 2)
                        dve.wait_ge(o_lo, t * TURN + lv + 1)
                        dve.reciprocal(rsum[:, :], psum[:, OBANK, LAT:2 * LAT]).then_inc(recip_done, 1)
                        dve.wait_ge(recip_done, t * TURN + lv + 1)
                        dve.tensor_tensor(oscaled[:, :], psum[:, OBANK, 0:LAT], rsum[:, :],
                                          ALU.mult).then_inc(o_scaled, 1)
                        dve.wait_ge(o_hi, t * TURN + lv + 1)
                        dve.scalar_tensor_tensor(out=OT_lo[:, g, :], in0=oscaled[:, :],
                                                 scalar=bias[:, 2, g:g + 1], in1=OT_hi[:, g, :].bitcast(F32),
                                                 op0=ALU.add, op1=ALU.subtract).then_inc(o_lo, 1)
                    if kind == "OUT":
                        dve.wait_ge(gen_filled, t * PER_TURN + n + 1)
                        dve.wait_ge(bo_added, t * (2 * QT) + QT * lv + x + 1)
                        dve.tensor_tensor(xb[:, x, :], psum[:, bank, :], xb[:, x, :],
                                          ALU.add).then_inc(gen_released, 1)

            dve.sem_inc(o_scaled, 1)
            dve.sem_inc(o_lo, 1)
            dve.memset(mask_r, 0.0).then_inc(masked, 1)
            dve.memset(QKS[96:98, 0, :, :].bitcast(F32), 1.0).then_inc(fixed_rows, 1)
            dve.memset(ones[:, :], 1.0).then_inc(ones_ready, 1)
            dve.wait_ge(masked, 1)
            dve.wait_ge(small_loaded, 32)
            dve.tensor_scalar(mask_r[:, 0:KEYS - LAT], mask_i, 0.0, MASKED, ALU.is_equal,
                              ALU.mult).then_inc(masked, 1)
            def split_lo(m):
                dve.wait_ge(w_hi, m + 1)
                dve.tensor_tensor(W_lo[:, m, :, :], staged(m), W_hi[:, m, :, :].bitcast(F32),
                                  ALU.subtract).then_inc(w_lo, 1)

            start_up(stages, split_lo)
            split_lo(2)
            split_lo(3)
            walk(dve, stages, REST[2:])

        @block.gpsimd
        def _(pool):
            def stages(t, todo):
                for kind, lv, x, n in todo:
                    slot, b = lv % RING, lv // FT
                    if kind in ("Q", "K"):
                        wait_apart(pool, started[0],
                                   (qk_hi, t * (2 * TURN) + 2 * lv + (1 if kind == "Q" else 2)))
                        cols, copy = (slice(0, LAT), srcB) if kind == "Q" else (slice(LAT, QK), srcC)
                        pool.tensor_copy(copy[:, cols], srcA[:, cols]).then_inc(qk_copied, 1)
                    if kind == "Q":
                        u0 = lv if isinstance(t, int) and t == 0 else lv + RING
                        if u0 >= RING:
                            wait_apart(pool, started[0],
                                       (st_filled, t * (TURN * PIECES) + PIECES * (lv - RING + 1)))
                        else:
                            pool.wait_ge(fixed_rows, lv + 1)
                            pool.wait_ge(mask_stored, 16 * HPG)
                        pool.dma_start(QKS[96:97, slot, :, LAT:QK].bitcast(F32),
                                       mask_d[t * 2 + b]).then_inc(mask_loaded[slot], 16)
                    if kind == "ADD":
                        pool.wait_ge(outs_done, t * TURN + lv + 1)
                        add_up(pool, t, lv, (2, 3), half_added_pool, added_pool)
                    if kind == "XB":
                        if isinstance(t, int) and t == 0 and lv == 0:
                            pool.wait_ge(bo_loaded, 16)
                        pool.wait_ge(x_loaded[x], t * 32 + 16 * (lv + 1))
                        pool.tensor_tensor(xb[:, x, :], xb[:, x, :], bo[:, :], ALU.add).then_inc(bo_added, 1)

            pool.sem_inc(started[0], 1)
            pool.memset(ident[:, :], 0.0).then_inc(ident_zero, 1)
            pool.wait_ge(ident_zero, 1)
            pool.affine_select(out=ident[:, :], in_=ident[:, :], compare_op=ALU.not_equal, fill=1.0,
                               base=0, pattern=[[-1, P]], channel_multiplier=1).then_inc(ident_ready, 1)
            pool.wait_ge(ident_ready, 1)
            for slot in range(1, RING):
                pool.wait_ge(fixed_rows, slot)
                pool.memset(QKS[96:98, slot, :, :].bitcast(F32), 1.0).then_inc(fixed_rows, 1)
            pool.wait_ge(fixed_rows, RING)
            walk(pool, stages)

        @block.sync
        def _(sp):
            def load_rows(t, b, ft):
                if not (isinstance(t, int) and t * 2 + b == 0 and ft < 2):
                    wait_apart(sp, started[1], (ht_lo, t * (2 * FT) + FT * b + ft - 1))
                sp.dma_start(stage[:, ft % 2, :],
                             hT[t * 2 + b, ft * P:(ft + 1) * P, :]).then_inc(ht_loaded[ft % 2], 16)

            def stages(t, todo):
                for kind, lv, x, n in todo:
                    slot = lv % RING
                    if kind == "HL":
                        load_rows(t, lv, x)
                    if kind == "STACK":
                        k_use = [m for k, v, _, m in todo if k == "K" and v == lv][0]
                        waits = [(qk_copied, t * (2 * TURN) + 2 * (lv + 1)),
                                 (gen_released, t * PER_TURN + k_use + 1)]
                        if lv >= RING or not (isinstance(t, int) and t == 0):
                            waits.append((st_filled, t * (TURN * PIECES) + PIECES * (lv - RING + 1)))
                        wait_apart(sp, started[1], *waits)
                        load_stack(sp, lv, (0, 1) if isinstance(t, int) and t * TURN + lv == 0 else range(HPG))
                    if kind == "M":
                        sp.wait_ge(gen_released, t * PER_TURN + n + 1)
                        sp.dma_start(QKS[97:98, slot, :, 0:LAT].bitcast(F32),
                                     mrow[:, :].bitcast(F32)).then_inc(max_loaded, 16)
                    if kind == "XL":
                        wait_apart(sp, started[1], (y_stored[x], t * 32 + 16 * lv + 16))
                        sp.dma_start(xb[:, x, :], latents[t * 2 + lv, x * P:(x + 1) * P, :])\
                            .then_inc(x_loaded[x], 16)
                    if kind == "OUT":
                        wait_apart(sp, started[1], (gen_released, t * PER_TURN + n + 1))
                        sp.dma_start(y_mid[t * 2 + lv, x * P:(x + 1) * P, :], xb[:, x, :])\
                            .then_inc(y_stored[x], 16)

            sp.sem_inc(started[1], 1)
            for q in range(QT):
                sp.sem_inc(y_stored[q], 16)
            def load_weight(m, w):
                sp.dma_start(staged(m), w.rearrange("(t p) n -> p t n", p=P)).then_inc(w_loaded[m], 16)

            sp.dma_start(mask_i, mask).then_inc(small_loaded, 16)
            sp.dma_start(bias[:, :, :], b_qkv).then_inc(small_loaded, 16)
            load_weight(0, w_q)
            stages(0, prologue[0:2])
            load_weight(1, w_k)
            sp.wait_ge(masked, 2)
            for j in range(HPG):
                sp.dma_start(mask_d[:, 0, j, :], mask_r).then_inc(mask_stored, 16)
            stages(0, prologue[2:8])
            load_weight(2, w_v)
            load_weight(3, w_out)
            sp.wait_ge(mask_stored, 16 * HPG)
            sp.dma_start(bo[:, :], b_out.to_broadcast((P, F))).then_inc(bo_loaded, 16)
            walk(sp, stages, REST)
            for q in range(QT):
                sp.wait_ge(y_stored[q], 16 * B + 16)


def mlp(nc, psum, y_mid, latents, w1, w2, b1, b2, norm_w, y_out):
    B, LAT, F = latents.shape
    HID = w1.shape[1]
    FT = F // P
    HT = HID // P
    QT = LAT // P
    PAIRS = B // 2
    TT = 2 * QT
    TOK = TT * P
    AHEAD = 2
    CHUNK = 2 * P
    CHUNKS = HID // CHUNK
    G = 4
    EPS = 1e-6
    M1_BANK, T_BANK, ACC = 0, 2, 4

    with ExitStack() as ctx:
        def sb(name, shape, dt=F32):
            return ctx.enter_context(nc.sbuf_tensor("m_" + name, shape, dt))

        def sem(name):
            return ctx.enter_context(nc.semaphore("m_" + name))

        W1_hi = sb("W1_hi", [P, FT, HID], F32R)
        W1_lo = sb("W1_lo", [P, FT, HID], F32R)
        W2_hi = sb("W2_hi", [P, HT, F], F32R)
        W2_lo = sb("W2_lo", [P, HT, F], F32R)
        stage1 = sb("stage1", [P, 2, FT, CHUNK])
        stage2 = sb("stage2", [P, 2, CHUNK // P, F])
        xt = sb("xt", [P, TT, F])
        square = sb("square", [P, QT, F])
        nT_hi = sb("nT_hi", [P, FT, TOK], F32R)
        nT_lo = sb("nT_lo", [P, FT, TOK], F32R)
        g = sb("g", [P, 2, TOK])
        g_hi = sb("g_hi", [P, G, TOK], F32R)
        g_lo = sb("g_lo", [P, G, TOK], F32R)
        res = sb("res", [P, TT, F])
        b2_rows = sb("b2_rows", [P, F])
        b1_col = sb("b1_col", [P, HT])
        norm_col = sb("norm_col", [P, FT])
        ident = sb("ident", [P, P])
        mean = sb("mean", [P, TT])
        root = sb("root", [P, TT])
        r0 = sb("r0", [P, TT])
        corr = sb("corr", [P, TT])
        rstd = sb("rstd", [P, TT])

        const_loaded = sem("const_loaded")
        ident_zero = sem("ident_zero")
        ident_ready = sem("ident_ready")
        w_loaded = [sem("w_loaded0"), sem("w_loaded1")]
        w_hi = sem("w_hi")
        w_lo = sem("w_lo")
        x_loaded = sem("x_loaded")
        res_loaded = sem("res_loaded")
        res_ready = sem("res_ready")
        stat = sem("stat")
        rooted = sem("rooted")
        normed = sem("normed")
        t_filled = sem("t_filled")
        t_hi = sem("t_hi")
        t_lo = sem("t_lo")
        m1_filled = sem("m1_filled")
        gelu_done = sem("gelu_done")
        g_hi_done = sem("g_hi_done")
        g_lo_done = sem("g_lo_done")
        m2_done = sem("m2_done")
        acc_filled = sem("acc_filled")
        acc_read = sem("acc_read")
        y_stored = sem("y_stored")
        started = sem("started")

        def pair_stages(first, last):
            out = []
            if first:
                out += [("L", -1), ("W", 0), ("N", -1)]
                out += [("T", ft - FT) for ft in range(FT)] + [("W", 1), ("M1", 0), ("M1", 1)]
            for f in range(HT):
                if first and f % 2 == 0 and f // 2 + 2 < CHUNKS:
                    out += [("W", f // 2 + 2)]
                if f == 1 and not last:
                    out += [("L", 0)]
                if f == 2:
                    out += [("R", 0)]
                if f == 6 and not last:
                    out += [("N", 0)]
                if f >= HT - 2 and not last:
                    out += [("T", 2 * (f - HT + 2)), ("T", 2 * (f - HT + 2) + 1)]
                out += [("M2", f)]
                if f + AHEAD < HT:
                    out += [("M1", f + AHEAD)]
            if not last:
                out += [("M1", HT), ("M1", HT + 1)]
            return out

        def walk(eng, stage_of):
            stage_of(0, pair_stages(True, False))
            with eng.Fori(1, PAIRS - 1) as t:
                stage_of(t, pair_stages(False, False))
            stage_of(PAIRS - 1, pair_stages(False, True))

        STATS = 11

        block = ctx.enter_context(nc.Block())

        @block.tensor
        def _(pe):
            def stages(t, todo):
                for kind, x in todo:
                    if kind == "T":
                        ft = x % FT
                        if x == -FT:
                            pe.wait_ge(ident_ready, 1)
                        if ft == 0:
                            pe.wait_ge(normed, t * TT + (TT if x < 0 else 2 * TT))
                        pe.wait_ge(t_lo, t * FT + x + FT + 1)
                        for i in range(TT):
                            mm = pe.transpose(psum[:, T_BANK + ft % 2, i * P:(i + 1) * P],
                                              xt[:, i, ft * P:(ft + 1) * P], ident[:, :])
                        mm.then_inc(t_filled, 1)
                    if kind == "M1":
                        f = x % HT
                        if x % HT == 0:
                            pe.wait_ge(t_lo, t * FT + FT * (x // HT + 1) + 2)
                        if isinstance(t, int) and t == 0 and x < HT and x % 2 == 0:
                            pe.wait_ge(w_lo, 2 * (x // 2 + 1))
                        pe.wait_ge(gelu_done, t * HT + x + 1)
                        fs = slice(f * P, (f + 1) * P)
                        for ft in range(FT):
                            mm = split_product(pe, psum[:, M1_BANK + x % 2, :],
                                               W1_hi[:, ft, fs], W1_lo[:, ft, fs],
                                               nT_hi[:, ft, :], nT_lo[:, ft, :], ft == 0, ft == FT - 1)
                        mm.then_inc(m1_filled, 1)
                    if kind == "M2":
                        pe.wait_ge(g_lo_done, t * HT + x + 1 + 2)
                        for i in range(TT):
                            if x == 0:
                                pe.wait_ge(acc_read, t * TT + i + 1)
                            ts = slice(i * P, (i + 1) * P)
                            mm = split_product(pe, psum[:, ACC + i, :], g_hi[:, x % G, ts], g_lo[:, x % G, ts],
                                               W2_hi[:, x, :], W2_lo[:, x, :], x == 0, x == HT - 1)
                            if x == HT - 1:
                                mm.then_inc(acc_filled, 1)
                        if x < HT - 1:
                            mm.then_inc(m2_done, 1)
                        else:
                            pe.wait_ge(acc_filled, t * TT + TT)
                            pe.sem_inc(m2_done, 1)

            pe.sem_inc(m2_done, G)
            walk(pe, stages)

        @block.scalar
        def _(act):
            act.wait_ge(const_loaded, 48)

            def stages(t, todo):
                for kind, x in todo:
                    if kind == "W":
                        act.wait_ge(w_loaded[x % 2], 32 * (x // 2 + 1))
                        act.activation(W1_hi[:, :, x * CHUNK:(x + 1) * CHUNK], stage1[:, x % 2, :, :],
                                       ACT.Copy).then_inc(w_hi, 1)
                        act.activation(W2_hi[:, 2 * x:2 * x + 2, :], stage2[:, x % 2, :, :],
                                       ACT.Copy).then_inc(w_hi, 1)
                    if kind == "N":
                        act.wait_ge(stat, t * STATS + STATS * (x + 1) + 5)
                        act.activation(root[:, :], mean[:, :], ACT.Sqrt).then_inc(rooted, 1)
                    if kind == "T":
                        ft = x % FT
                        act.wait_ge(t_filled, t * FT + x + FT + 1)
                        act.activation(nT_hi[:, ft, :], psum[:, T_BANK + ft % 2, :], ACT.Identity,
                                       scale=norm_col[:, ft:ft + 1]).then_inc(t_hi, 1)
                    if kind == "M1":
                        act.wait_ge(m1_filled, t * HT + x + 1)
                        act.wait_ge(g_lo_done, t * HT + x + 1)
                        act.activation(g[:, x % 2, :], psum[:, M1_BANK + x % 2, :], ACT.Gelu_apprx_tanh,
                                       bias=b1_col[:, x % HT:x % HT + 1]).then_inc(gelu_done, 1)
                        act.wait_ge(gelu_done, t * HT + x + 1 + 2)
                        act.wait_ge(m2_done, t * HT + x + 1)
                        act.activation(g_hi[:, x % G, :], g[:, x % 2, :], ACT.Copy).then_inc(g_hi_done, 1)

            act.sem_inc(gelu_done, 2)
            walk(act, stages)

        @block.vector
        def _(dve):
            dve.wait_ge(const_loaded, 48)

            def stages(t, todo):
                for kind, x in todo:
                    if kind == "N":
                        p = x + 1
                        s = t * STATS + STATS * p
                        for b in range(2):
                            dve.wait_ge(x_loaded, t * 32 + 32 * p + 32)
                            if b == 1:
                                dve.wait_ge(stat, s + 2)
                            bs = slice(QT * b, QT * (b + 1))
                            dve.tensor_tensor(square[:, :, :], xt[:, bs, :], xt[:, bs, :],
                                              ALU.mult).then_inc(stat, 1)
                            dve.wait_ge(stat, s + 2 * b + 1)
                            dve.tensor_reduce(mean[:, bs], square[:, :, :], AX_X, ALU.add).then_inc(stat, 1)
                        dve.wait_ge(stat, s + 4)
                        dve.tensor_scalar(mean[:, :], mean[:, :], 1.0 / F, EPS, ALU.mult,
                                          ALU.add).then_inc(stat, 1)
                        dve.wait_ge(rooted, t + p + 1)
                        dve.reciprocal(r0[:, :], root[:, :]).then_inc(stat, 1)
                        dve.wait_ge(stat, s + 6)
                        dve.tensor_tensor(corr[:, :], mean[:, :], r0[:, :], ALU.mult).then_inc(stat, 1)
                        dve.wait_ge(stat, s + 7)
                        dve.tensor_tensor(corr[:, :], corr[:, :], r0[:, :], ALU.mult).then_inc(stat, 1)
                        dve.wait_ge(stat, s + 8)
                        dve.tensor_scalar(corr[:, :], corr[:, :], -0.5, 1.5, ALU.mult,
                                          ALU.add).then_inc(stat, 1)
                        dve.wait_ge(stat, s + 9)
                        dve.tensor_tensor(rstd[:, :], r0[:, :], corr[:, :], ALU.mult).then_inc(stat, 1)
                        dve.wait_ge(stat, s + 10)
                        for i in range(TT):
                            dve.tensor_scalar(xt[:, i, :], xt[:, i, :], rstd[:, i:i + 1], None,
                                              ALU.mult).then_inc(normed, 1)
                        dve.wait_ge(normed, t * TT + TT * (p + 1))
                        dve.sem_inc(stat, 1)
                    if kind == "T":
                        ft = x % FT
                        dve.wait_ge(t_hi, t * FT + x + FT + 1)
                        dve.scalar_tensor_tensor(out=nT_lo[:, ft, :], in0=psum[:, T_BANK + ft % 2, :],
                                                 scalar=norm_col[:, ft:ft + 1],
                                                 in1=nT_hi[:, ft, :].bitcast(F32), op0=ALU.mult,
                                                 op1=ALU.subtract).then_inc(t_lo, 1)
                    if kind == "M1":
                        dve.wait_ge(g_hi_done, t * HT + x + 1)
                        dve.tensor_tensor(g_lo[:, x % G, :], g[:, x % 2, :],
                                          g_hi[:, x % G, :].bitcast(F32), ALU.subtract).then_inc(g_lo_done, 1)
                    if kind == "M2" and x == HT - 1:
                        dve.wait_ge(res_ready, t + 1)
                        for i in range(TT):
                            dve.wait_ge(acc_filled, t * TT + i + 1)
                            dve.tensor_tensor(res[:, i, :], psum[:, ACC + i, :], res[:, i, :],
                                              ALU.add).then_inc(acc_read, 1)

            dve.sem_inc(t_lo, 2)
            dve.sem_inc(g_lo_done, 2)
            dve.sem_inc(acc_read, TT)
            walk(dve, stages)

        @block.gpsimd
        def _(pool):
            pool.memset(ident[:, :], 0.0).then_inc(ident_zero, 1)
            pool.wait_ge(ident_zero, 1)
            pool.affine_select(out=ident[:, :], in_=ident[:, :], compare_op=ALU.not_equal, fill=1.0,
                               base=0, pattern=[[-1, P]], channel_multiplier=1).then_inc(ident_ready, 1)
            pool.wait_ge(const_loaded, 48)

            def stages(t, todo):
                for kind, x in todo:
                    if kind == "W":
                        pool.wait_ge(w_hi, 2 * x + 1)
                        cs = slice(x * CHUNK, (x + 1) * CHUNK)
                        pool.tensor_tensor(W1_lo[:, :, cs], stage1[:, x % 2, :, :],
                                          W1_hi[:, :, cs].bitcast(F32), ALU.subtract).then_inc(w_lo, 1)
                        pool.wait_ge(w_hi, 2 * x + 2)
                        pool.tensor_tensor(W2_lo[:, 2 * x:2 * x + 2, :], stage2[:, x % 2, :, :],
                                          W2_hi[:, 2 * x:2 * x + 2, :].bitcast(F32),
                                          ALU.subtract).then_inc(w_lo, 1)
                    if kind == "R":
                        for i in range(TT):
                            pool.wait_ge(res_loaded, t * 32 + 32)
                            inst = pool.tensor_tensor(res[:, i, :], res[:, i, :], b2_rows[:, :], ALU.add)
                            if i == TT - 1:
                                inst.then_inc(res_ready, 1)

            walk(pool, stages)

        @block.sync
        def _(sp):
            sp.dma_start(b1_col[:, :], b1).then_inc(const_loaded, 16)
            sp.dma_start(norm_col[:, :], norm_w).then_inc(const_loaded, 16)
            sp.dma_start(b2_rows[:, :], b2.to_broadcast((P, F))).then_inc(const_loaded, 16)
            w1_rows = w1.rearrange("(t p) n -> p t n", p=P)
            w2_rows = w2.rearrange("(t p) n -> p t n", p=P)

            def stages(t, todo):
                for kind, x in todo:
                    if kind == "W":
                        if x >= 2:
                            sp.wait_ge(w_lo, 2 * (x - 1))
                        sp.dma_start(stage1[:, x % 2, :, :], w1_rows[:, :, x * CHUNK:(x + 1) * CHUNK])\
                            .then_inc(w_loaded[x % 2], 16)
                        sp.dma_start(stage2[:, x % 2, :, :], w2_rows[:, 2 * x:2 * x + 2, :])\
                            .then_inc(w_loaded[x % 2], 16)
                    if kind == "L":
                        if x == 0:
                            wait_apart(sp, started, (t_filled, t * FT + FT))
                        for b in range(2):
                            sp.dma_start(xt[:, QT * b:QT * (b + 1), :],
                                         y_mid[(t + x + 1) * 2 + b].rearrange("(q p) n -> p q n", p=P))\
                                .then_inc(x_loaded, 16)
                    if kind == "R":
                        wait_apart(sp, started, (y_stored, t * 32 + 32))
                        for b in range(2):
                            sp.dma_start(res[:, QT * b:QT * (b + 1), :],
                                         latents[t * 2 + b].rearrange("(q p) n -> p q n", p=P))\
                                .then_inc(res_loaded, 16)
                    if kind == "M2" and x == HT - 1:
                        for b in range(2):
                            wait_apart(sp, started, (acc_read, t * TT + QT * (b + 1) + TT))
                            sp.dma_start(y_out[t * 2 + b].rearrange("(q p) n -> p q n", p=P),
                                         res[:, QT * b:QT * (b + 1), :]).then_inc(y_stored, 16)

            sp.sem_inc(started, 1)
            sp.sem_inc(y_stored, 32)
            walk(sp, stages)
            sp.wait_ge(y_stored, 32 * PAIRS + 32)


def attention1(nc, psum, query, context, w_q, w_k, w_v, w_out, b_out, y_out):
    B, C, L = query.shape
    CT = C // P
    KT = L // P
    D = 16
    HEADS = C // D
    ROWS = 32
    HPG = P // ROWS
    GROUPS = HEADS // HPG
    SCALE = D ** -0.5
    RING = 4
    TURN = 2 * GROUPS
    TURNS = B // 2
    HALVES = 2
    HKT = KT // HALVES
    NST = HALVES * HPG
    PIECES = NST * HKT
    ST_BANKS = 3
    OPS = 96
    GEN = (3, 4, 5, 6)
    OBANK = 7

    with ExitStack() as ctx:
        def sb(name, shape, dt=F32):
            return ctx.enter_context(nc.sbuf_tensor("a1_" + name, shape, dt))

        def sem(name):
            return ctx.enter_context(nc.semaphore("a1_" + name))

        W_hi = sb("W_hi", [P, 3, CT, C], F32R)
        W_lo = sb("W_lo", [P, 3, CT, C], F32R)
        Wo_hi = sb("Wo_hi", [P, CT, C], F32R)
        Wo_lo = sb("Wo_lo", [P, CT, C], F32R)
        QKS = sb("QKS", [P, RING, HPG, 2 * L], F32R)
        PT = sb("PT", [P, NST, HKT * L])
        V = sb("V", [P, 2, KT, GROUPS // 2, 2, HPG, ROWS])
        stage = sb("stage", [P, 2, CT, L])
        X_hi = sb("X_hi", [P, 2, CT, L], F32R)
        X_lo = sb("X_lo", [P, 2, CT, L], F32R)
        res = sb("res", [P, CT, L])
        O = sb("O", [P, GROUPS, L])
        OP_hi = sb("OP_hi", [P, CT, L], F32R)
        OP_lo = sb("OP_lo", [P, CT, L], F32R)
        srcA = sb("srcA", [P, 2 * L], F32R)
        srcB = sb("srcB", [P, 2 * L], F32R)
        srcC = sb("srcC", [P, 2 * L], F32R)
        recips = sb("recips", [P, 2, L])
        flat = sb("flat", [P, 2 * HPG * L // P])
        mrow = sb("mrow", [HPG, L], F32R)
        mx = sb("mx", [P, KT, HPG])
        ident = sb("ident", [P, P])
        bo = sb("bo", [P, CT])
        sums_d = nc.dram_tensor("sums_rows", (2, HPG, L), F32, kind="Internal").ap()
        recips_d = nc.dram_tensor("recips_rows", (2, HPG, L), F32, kind="Internal").ap()

        stagew = PT[:, 0:3, 0:CT * C].rearrange("p m (t n) -> p m t n", t=CT)
        stageo = PT[:, 3, 0:CT * C].rearrange("p (g n) -> p g n", g=CT)

        w_loaded = [sem(f"w_loaded{m}") for m in range(4)]
        bo_loaded = sem("bo_loaded")
        w_hi = sem("w_hi")
        w_lo = sem("w_lo")
        ident_zero = sem("ident_zero")
        ident_ready = sem("ident_ready")
        ones_ready = sem("ones_ready")
        fixed_rows = sem("fixed_rows")
        gen_filled = sem("gen_filled")
        gen_released = sem("gen_released")
        x_loaded = sem("x_loaded")
        x_hi = sem("x_hi")
        x_lo = sem("x_lo")
        qk_hi = sem("qk_hi")
        qk_copied = sem("qk_copied")
        stack_loaded = [sem(f"stack_loaded{r}") for r in range(RING)]
        max_loaded = sem("max_loaded")
        st_filled = sem("st_filled")
        exp_done = sem("exp_done")
        av_done = sem("av_done")
        o_copied = sem("o_copied")
        sums_stored = sem("sums_stored")
        sums_loaded = sem("sums_loaded")
        recip_done = sem("recip_done")
        recips_stored = sem("recips_stored")
        recips_loaded = sem("recips_loaded")
        o_scaled = sem("o_scaled")
        op_hi = sem("op_hi")
        op_lo = sem("op_lo")
        recips_zero = sem("recips_zero")
        res_loaded = sem("res_loaded")
        y_stored = sem("y_stored")
        started = [sem("pool_started"), sem("sp_started")]
        STACK = 16 * 3 * HPG
        LAPS = TURN // RING

        USES = {"S": 2, "Q": 1, "K": 1, "M": 1, "V": 1, "OUT": 1}

        AHEAD = 3
        PROLOGUE = [("XL", 0, 0), ("X", 0, 0), ("X", 0, 1), ("X", 0, 2), ("X", 0, 3), ("Q", 0, 0), ("K", 0, 0), ("STACK", 0, 0), ("STACK", 0, 2)]
        PROLOGUE += [("V", 0, n) for n in range(KT)] + [("XL", 1, 0)]
        PROLOGUE += [("S", 0, i) for i in range(NST)] + [("Q", 1, 0), ("K", 1, 0), ("M", 0, 0)]
        PROLOGUE += [("STACK", 1, 0), ("STACK", 1, 1)] + [("S", 1, i) for i in range(AHEAD)]
        PROLOGUE += [("STACK", 1, 2), ("STACK", 1, 3)]

        def step(lu, first, last):
            g, b = lu % GROUPS, lu // GROUPS
            units = TURN if last else 2 * TURN
            more = not (last and lu >= GROUPS)
            before = not (first and lu == 0)
            out = []
            if lu % 2 == 0 and lu + 3 < units and before:
                out += [("STACK", lu // 2 + 1, 2)]
            out += [("RL", b - 1, 0)] * (g == 0 and not (first and b == 0))
            between = {2: [("V", b + 1, 2), ("V", b + 1, 3)] * more}.get(g, [])
            if lu % 2 == 1:
                between = [("Q", (lu + 3) // 2, 0), ("K", (lu + 3) // 2, 0)] * (lu + 3 < units)
            if g == 3 and not (first and b == 0):
                between += [("OUT", b - 1, 0), ("OUT", b - 1, 1)]
            for i in range(NST):
                out += [("ST", lu, i)]
                if i < 2 and before:
                    out += [("AV", lu - 1, i + 2)]
                if i == 5:
                    out += [("AV", lu, 0)] + [("M", lu + 1, 0)] * (lu + 1 < units)
                    if lu % 2 == 1 and lu + 3 < units:
                        out += [("STACK", (lu + 3) // 2, 0), ("STACK", (lu + 3) // 2, 1)]
                    if lu % 2 == 0 and lu + 3 < units and before:
                        out += [("STACK", lu // 2 + 1, 3)]
                u, part = lu + 1 + (i + AHEAD) // NST, (i + AHEAD) % NST
                if u < units:
                    out += [("S", u, part)]
                out += [("X", b + 1, i - 1)] * (g == 0 and more and 1 <= i < 5)
                if i == 2:
                    out += between[0:1]
                    out += [("OC", lu // 2 - 2, 0)] * (lu % 2 == 0 and not (first and lu < 4))
                if i == 3:
                    out += between[1:2]
                if i == 5:
                    out += between[2:3] + [("R", lu // 2 - 1, 0)] * (lu % 2 == 0 and before)
                if i == 6:
                    out += [("AV", lu, 1)]
                if i == 7:
                    out += between[3:4]
                    out += [("OH", lu // 2 - 1, 0)] * (lu % 2 == 1 and not (first and lu == 1))
                    out += [("SC", lu // 2 - 1, 0)] * (lu % 2 == 0 and before)
            if g == 0 and more:
                out += [("V", b + 1, 0), ("V", b + 1, 1)]
            if g == 2:
                out += [("XL", b + 2, 0)] * (not last)
            return out

        def counted(stages, n):
            out = []
            for stage in stages:
                out.append((*stage, n))
                n += USES.get(stage[0], 0)
            return out, n

        prologue, n0 = counted(PROLOGUE, 0)
        first_turn, n1 = counted([s for lu in range(TURN) for s in step(lu, True, False)], n0)
        PER_TURN = sum(USES.get(s[0], 0) for lu in range(TURN) for s in step(lu, False, False))
        assert PER_TURN % len(GEN) == 0
        turn, _ = counted([s for lu in range(TURN) for s in step(lu, False, False)], n1 - PER_TURN)
        last_turn, _ = counted([s for lu in range(TURN) for s in step(lu, False, True)]
                               + [("AV", TURN - 1, 2), ("AV", TURN - 1, 3), ("OC", TURN // 2 - 2, 0),
                                  ("R", TURN // 2 - 1, 0), ("RL", 1, 0), ("SC", TURN // 2 - 1, 0),
                                  ("OH", TURN // 2 - 1, 0), ("OC", TURN // 2 - 1, 0),
                                  ("OUT", 1, 0), ("OUT", 1, 1)], n1 - PER_TURN)

        def walk(eng, stage_of, before=prologue):
            stage_of(0, before + first_turn)
            with eng.Fori(1, TURNS - 1) as t:
                stage_of(t, turn)
            stage_of(TURNS - 1, last_turn)

        block = ctx.enter_context(nc.Block())

        def split_weight(m):
            if m == 3:
                return stageo, Wo_hi[:, :, :], Wo_lo[:, :, :]
            return stagew[:, m, :, :], W_hi[:, m, :, :], W_lo[:, m, :, :]

        def fill(eng, slot):
            eng.memset(QKS[:, slot, :, 0:L].bitcast(F32), 0.0)
            eng.memset(QKS[:, slot, :, L:2 * L].bitcast(F32), 1.0).then_inc(fixed_rows, 1)

        def load_stack(eng, u, part):
            for j in (2 * part, 2 * part + 1):
                rows = slice((u % 2 * HPG + j) * D, (u % 2 * HPG + j + 1) * D)
                for r, src in enumerate((srcA, srcB, srcC)):
                    eng.dma_start(QKS[r * D:(r + 1) * D, u % RING, j, :].bitcast(F32),
                                  src[rows, :].bitcast(F32)).then_inc(stack_loaded[u % RING], 16)

        @block.tensor
        def _(pe):
            def claim(t, n):
                if n >= len(GEN) or not isinstance(t, int) or t > 0:
                    pe.wait_ge(gen_released, t * PER_TURN + n - len(GEN) + 1)
                return GEN[n % len(GEN)]

            def stages(t, todo):
                for kind, v, x, n in todo:
                    if kind in ("Q", "K", "V") and x == 0:
                        b = v if kind == "V" else v // 2
                        pe.wait_ge(x_lo, t * 8 + 4 * (b + 1))
                    if isinstance(t, int) and t == 0 and v == 0 and x == 0 and kind in ("Q", "K", "V"):
                        pe.wait_ge(w_lo, "QKV".index(kind) + 1)
                    if isinstance(t, int) and t == 0 and v < RING and x == 0 and kind == "S":
                        pe.wait_ge(fixed_rows, v + 1)
                    if kind in ("Q", "K"):
                        m = 0 if kind == "Q" else 1
                        cs = slice((v % 2) * P, (v % 2 + 1) * P)
                        bank = claim(t, n)
                        for ct in range(CT):
                            mm = split_product(pe, psum[:, bank, :], W_hi[:, m, ct, cs], W_lo[:, m, ct, cs],
                                               X_hi[:, m, ct, :], X_lo[:, m, ct, :], ct == 0, ct == CT - 1)
                        mm.then_inc(gen_filled, 1)
                    if kind == "V":
                        ks = slice(x * P, (x + 1) * P)
                        bank = claim(t, n)
                        for ct in range(CT):
                            mm = split_product(pe, psum[:, bank, 0:C], X_hi[:, 1, ct, ks], X_lo[:, 1, ct, ks],
                                               W_hi[:, 2, ct, :], W_lo[:, 2, ct, :], ct == 0, ct == CT - 1)
                        mm.then_inc(gen_filled, 1)
                    if kind == "S":
                        slot = v % RING
                        if x == 0:
                            pe.wait_ge(stack_loaded[slot], t * (LAPS * STACK) + (v // RING + 1) * STACK)
                        for k in range(2):
                            q = 2 * (x % 2) + k
                            bank = claim(t, n + k)
                            pe.matmul(psum[:, bank, :], QKS[0:OPS, slot, x // 2, q * P:(q + 1) * P],
                                      QKS[0:OPS, slot, x // 2, L:2 * L], start=True,
                                      stop=True).then_inc(gen_filled, 1)
                    if kind == "M":
                        last_s = max(m for k, u, _, m in todo if k == "S" and u == v) + 2
                        pe.wait_ge(gen_released, t * PER_TURN + last_s)
                        if isinstance(t, int) and t * TURN + v == 0:
                            pe.wait_ge(ident_ready, 1)
                        bank = claim(t, n)
                        for q in range(KT):
                            mm = pe.transpose(psum[0:HPG, bank, q * P:(q + 1) * P], mx[:, q, :],
                                              ident[:, :])
                        mm.then_inc(gen_filled, 1)
                    if kind == "ST":
                        slot, half, j = v % RING, x // HPG, x % HPG
                        if x == 0:
                            pe.wait_ge(max_loaded, t * (16 * TURN) + 16 * (v + 1))
                        for k in range(HKT):
                            kt, s = half * HKT + k, PIECES * v + HKT * x + k
                            if not (isinstance(t, int) and t == 0):
                                pe.wait_ge(exp_done, t * (TURN * PIECES) + (s - ST_BANKS + 1 if s >= ST_BANKS
                                                                            else 0))
                            elif s >= ST_BANKS:
                                pe.wait_ge(exp_done, s - ST_BANKS + 1)
                            pe.matmul(psum[:, s % ST_BANKS, :],
                                      QKS[0:OPS + 1, slot, j, L + kt * P:L + (kt + 1) * P],
                                      QKS[0:OPS + 1, slot, j, 0:L], start=True,
                                      stop=True).then_inc(st_filled, 1)
                    if kind == "AV":
                        g, b = v % GROUPS, v // GROUPS
                        half, k = x // HKT, x % HKT
                        if k == 0:
                            pe.wait_ge(exp_done, t * (TURN * PIECES) + PIECES * v + HPG * HKT * (half + 1))
                        if x == 0:
                            pe.wait_ge(o_copied, t * TURN + v + 1)
                        for j in range(HPG):
                            mm = pe.matmul(psum[j * ROWS:(j + 1) * ROWS, OBANK, :],
                                           V[:, b % 2, x, g // 2, g % 2, j, :],
                                           PT[:, half * HPG + j, k * L:(k + 1) * L],
                                           start=(x == 0), stop=(x == KT - 1), skip_group_check=True)
                        if k == HKT - 1:
                            mm.then_inc(av_done, 1)
                    if kind == "OUT":
                        if x == 0:
                            pe.wait_ge(op_lo, t * (TURN // 2) + CT * (v + 1))
                        cs = slice(x * P, (x + 1) * P)
                        bank = claim(t, n)
                        for c in range(CT):
                            mm = split_product(pe, psum[:, bank, :], Wo_hi[:, c, cs], Wo_lo[:, c, cs],
                                               OP_hi[:, c, :], OP_lo[:, c, :], c == 0, c == CT - 1)
                        mm.then_inc(gen_filled, 1)

            pe.sem_inc(av_done, 2)
            walk(pe, stages)

        @block.scalar
        def _(act):
            def stages(t, todo):
                for kind, v, x, n in todo:
                    if kind == "X":
                        act.wait_ge(x_loaded, t * 64 + 32 * (v + 1))
                        if n > 0:
                            act.wait_ge(gen_filled, t * PER_TURN + n)
                        act.activation(X_hi[:, x // CT, x % CT, :], stage[:, x // CT, x % CT, :], ACT.Copy).then_inc(x_hi, 1)
                    if kind in ("Q", "K"):
                        act.wait_ge(gen_filled, t * PER_TURN + n + 1)
                        if kind == "Q" and v > 0:
                            for u in (2 * v - 2, 2 * v - 1):
                                act.wait_ge(stack_loaded[u % RING], t * (LAPS * STACK)
                                            + (u // RING + 1) * STACK)
                        cols = slice(0, L) if kind == "Q" else slice(L, 2 * L)
                        act.activation(srcA[:, cols], psum[:, GEN[n % len(GEN)], :],
                                       ACT.Copy).then_inc(qk_hi, 1)
                    if kind == "ST":
                        if isinstance(t, int) and t * TURN + v == 0 and x == 0:
                            act.wait_ge(w_lo, 4)
                        for k in range(HKT):
                            s = PIECES * v + HKT * x + k
                            act.wait_ge(st_filled, t * (TURN * PIECES) + s + 1)
                            if x % HPG == 0 and k == 0:
                                act.wait_ge(av_done, t * (2 * TURN) + 2 * v + x // HPG + 1)
                            act.activation(PT[:, x, k * L:(k + 1) * L], psum[:, s % ST_BANKS, :],
                                           ACT.Exp, scale=SCALE).then_inc(exp_done, 1)
                    if kind == "AV" and x == KT - 1:
                        act.wait_ge(av_done, t * (2 * TURN) + 2 * v + 2 + 2)
                        if not isinstance(t, int) or t * TURN + v >= GROUPS:
                            act.wait_ge(op_lo, t * (TURN // 2) + v // 2 - GROUPS // 2 + 1)
                        act.activation(O[:, v % GROUPS, :], psum[:, OBANK, :],
                                       ACT.Copy).then_inc(o_copied, 1)
                    if kind == "OC":
                        act.wait_ge(o_scaled, t * (3 * TURN // 2) + 3 * (v + 1))
                        act.activation(OP_hi[:, v % CT, :], O[:, 2 * v % GROUPS, :],
                                       ACT.Copy).then_inc(op_hi, 1)

            act.sem_inc(o_copied, 1)
            for m in range(4):
                staged, hi, _ = split_weight(m)
                act.wait_ge(w_loaded[m], 16)
                act.activation(hi, staged, ACT.Copy).then_inc(w_hi, 1)
                if m == 0:
                    stages(0, prologue[1:5])
            stages(0, prologue[5:7])
            act.wait_ge(qk_copied, 2)
            act.wait_ge(gen_released, 2)
            for u in range(2):
                act.wait_ge(fixed_rows, u + 1)
                load_stack(act, u, 1)
            walk(act, stages, prologue[7:])

        @block.vector
        def _(dve):
            def stages(t, todo):
                for kind, v, x, n in todo:
                    bank = GEN[n % len(GEN)]
                    if kind in ("Q", "K"):
                        dve.wait_ge(qk_hi, t * TURN + 2 * v + (1 if kind == "Q" else 2))
                        cols, lo = (slice(0, L), srcC) if kind == "Q" else (slice(L, 2 * L), srcB)
                        dve.tensor_tensor(lo[:, cols], psum[:, bank, :], srcA[:, cols].bitcast(F32),
                                          ALU.subtract).then_inc(gen_released, 1)
                    if kind == "V":
                        dve.wait_ge(gen_filled, t * PER_TURN + n + 1)
                        values = psum[:, bank, 0:C].rearrange("p (g w j d) -> p g w j d", w=2, j=HPG, d=D)
                        dve.tensor_copy(V[:, v % 2, x, :, 0, :, 0:D], values[:, :, 0])
                        dve.tensor_copy(V[:, v % 2, x, :, 1, :, D:ROWS], values[:, :, 1])\
                            .then_inc(gen_released, 1)
                    if kind == "S":
                        for k in range(2):
                            q = 2 * (x % 2) + k
                            dve.wait_ge(gen_filled, t * PER_TURN + n + k + 1)
                            dve.tensor_reduce(mx[:, q, x // 2:x // 2 + 1], psum[:, GEN[(n + k) % len(GEN)], :],
                                              AX_X, ALU.max).then_inc(gen_released, 1)
                    if kind == "M":
                        dve.wait_ge(gen_filled, t * PER_TURN + n + 1)
                        if v > 0:
                            dve.wait_ge(max_loaded, t * (16 * TURN) + 16 * v)
                        dve.tensor_scalar(mrow[:, :], psum[0:HPG, bank, :], -1.0, None,
                                          ALU.mult).then_inc(gen_released, 1)
                    if kind == "SC":
                        dve.wait_ge(sums_loaded, t * (16 * TURN // 2) + 16 * (v + 1))
                        dve.reciprocal(flat[:, :], flat[:, :]).then_inc(recip_done, 1)
                    if kind == "OUT":
                        if x == 0:
                            dve.wait_ge(res_loaded, t * 32 + 16 * (v + 1))
                        dve.wait_ge(gen_filled, t * PER_TURN + n + 1)
                        dve.scalar_tensor_tensor(out=res[:, x, :], in0=psum[:, bank, :],
                                                 scalar=bo[:, x:x + 1], in1=res[:, x, :], op0=ALU.add,
                                                 op1=ALU.add).then_inc(gen_released, 1)

            fill(dve, 0)
            for m in range(4):
                staged, hi, lo = split_weight(m)
                dve.wait_ge(w_hi, m + 1)
                dve.tensor_tensor(lo, staged, hi.bitcast(F32), ALU.subtract).then_inc(w_lo, 1)
            dve.wait_ge(bo_loaded, 16)
            dve.wait_ge(ones_ready, 1)
            walk(dve, stages)

        @block.gpsimd
        def _(pool):
            def stages(t, todo):
                for kind, v, x, n in todo:
                    if kind == "X":
                        m, ct = x // CT, x % CT
                        pool.wait_ge(x_hi, t * 8 + 4 * v + x + 1)
                        pool.tensor_tensor(X_lo[:, m, ct, :], stage[:, m, ct, :],
                                           X_hi[:, m, ct, :].bitcast(F32), ALU.subtract).then_inc(x_lo, 1)
                    if kind in ("Q", "K"):
                        wait_apart(pool, started[0],
                                   (qk_hi, t * TURN + 2 * v + (1 if kind == "Q" else 2)))
                        cols, copy = (slice(0, L), srcB) if kind == "Q" else (slice(L, 2 * L), srcC)
                        pool.tensor_copy(copy[:, cols], srcA[:, cols]).then_inc(qk_copied, 1)
                    if kind == "AV" and x == KT - 1:
                        waits = [(o_copied, t * TURN + v + 1 + 1)]
                        if not isinstance(t, int) or t * TURN + v >= 2:
                            waits.append((sums_loaded, t * (16 * TURN // 2) + 16 * (v // 2)))
                        wait_apart(pool, started[0], *waits)
                        pool.dma_start(sums_d[v % 2], O[D * (1 - v % 2):P:ROWS, v % GROUPS, :]).then_inc(sums_stored, 16)
                    if kind == "R":
                        wait_apart(pool, started[0], (sums_stored, t * (16 * TURN) + 32 * (v + 1)))
                        pool.dma_start(flat[:, :], sums_d.rearrange("u j (c n) -> (u j c) n", n=flat.shape[1]))\
                            .then_inc(sums_loaded, 16)
                    if kind == "SC":
                        wait_apart(pool, started[0], (recip_done, t * (TURN // 2) + v + 1))
                        pool.dma_start(recips_d.rearrange("u j (c n) -> (u j c) n", n=flat.shape[1]),
                                       flat[:, :]).then_inc(recips_stored, 16)
                        wait_apart(pool, started[0], (recips_stored, t * (16 * TURN // 2) + 16 * (v + 1)))
                        for w in range(2):
                            for j in range(HPG):
                                row = j * ROWS + w * D
                                pool.dma_start(recips[row:row + D, w, :],
                                               recips_d[w, j:j + 1, :].to_broadcast((D, L)))\
                                    .then_inc(recips_loaded, 16)
                    if kind == "OH":
                        even, odd = 2 * v % GROUPS, (2 * v + 1) % GROUPS
                        scaled = t * (3 * TURN // 2) + 3 * v
                        wait_apart(pool, started[0],
                                   (recips_loaded, t * (128 * TURN // 2) + 128 * (v + 1)))
                        for u, w in ((even, 0), (odd, 1)):
                            pool.tensor_tensor(O[:, u, :], O[:, u, :], recips[:, w, :],
                                               ALU.mult).then_inc(o_scaled, 1)
                        pool.wait_ge(o_scaled, scaled + 2)
                        pool.tensor_tensor(O[:, even, :], O[:, even, :], O[:, odd, :],
                                           ALU.add).then_inc(o_scaled, 1)
                    if kind == "OC":
                        even = 2 * v % GROUPS
                        pool.wait_ge(op_hi, t * (TURN // 2) + v + 1)
                        pool.tensor_tensor(OP_lo[:, v % CT, :], O[:, even, :],
                                           OP_hi[:, v % CT, :].bitcast(F32),
                                           ALU.subtract).then_inc(op_lo, 1)

            pool.sem_inc(started[0], 1)
            stages(0, prologue[1:5])
            pool.memset(V[:, :, :, :, :, :, :], 1.0).then_inc(ones_ready, 1)
            pool.memset(recips[:, :, :], 0.0).then_inc(recips_zero, 1)
            pool.memset(ident[:, :], 0.0).then_inc(ident_zero, 1)
            pool.wait_ge(ident_zero, 1)
            pool.affine_select(out=ident[:, :], in_=ident[:, :], compare_op=ALU.not_equal, fill=1.0,
                               base=0, pattern=[[-1, P]], channel_multiplier=1).then_inc(ident_ready, 1)
            stages(0, prologue[5:7])
            pool.wait_ge(fixed_rows, 1)
            for slot in range(1, RING):
                fill(pool, slot)
            pool.wait_ge(recips_zero, 1)
            walk(pool, stages, prologue[7:])

        @block.sync
        def _(sp):
            def stages(t, todo):
                for kind, v, x, n in todo:
                    if kind == "XL":
                        if not (isinstance(t, int) and t * 2 + v == 0):
                            wait_apart(sp, started[1], (x_lo, t * 8 + 4 * v))
                        for m, src in enumerate((query, context)):
                            sp.dma_start(stage[:, m, :, :], src[t * 2 + v].rearrange("(c p) n -> p c n", p=P))\
                                .then_inc(x_loaded, 16)
                    if kind == "STACK":
                        u = 2 * v + x // 2
                        if x == 0:
                            wait_apart(sp, started[1], (qk_copied, t * TURN + 2 * (v + 1)),
                                       (gen_released, t * PER_TURN + n))
                        if not isinstance(t, int) or t * TURN + u >= RING:
                            wait_apart(sp, started[1],
                                       (st_filled, t * (TURN * PIECES) + PIECES * (u - RING + 1)))
                        else:
                            sp.wait_ge(fixed_rows, u + 1)
                        load_stack(sp, u, x % 2)
                    if kind == "M":
                        sp.wait_ge(gen_released, t * PER_TURN + n + 1)
                        sp.dma_start(QKS[OPS:OPS + 1, v % RING, :, 0:L].bitcast(F32),
                                     mrow[:, :].bitcast(F32)).then_inc(max_loaded, 16)
                    if kind == "RL":
                        wait_apart(sp, started[1], (y_stored, t * 32 + 16 * v + 16))
                        sp.dma_start(res[:, :, :], query[t * 2 + v].rearrange("(c p) n -> p c n", p=P))\
                            .then_inc(res_loaded, 16)
                    if kind == "OUT" and x == 1:
                        wait_apart(sp, started[1], (gen_released, t * PER_TURN + n + 1))
                        sp.dma_start(y_out[t * 2 + v].rearrange("(c p) n -> p c n", p=P), res[:, :, :])\
                            .then_inc(y_stored, 16)

            sp.sem_inc(started[1], 1)
            sp.sem_inc(y_stored, 16)
            sp.dma_start(stagew[:, 0, :, :], w_q.rearrange("(t p) n -> p t n", p=P)).then_inc(w_loaded[0], 16)
            stages(0, prologue[0:1])
            for m, w in ((1, w_k), (2, w_v)):
                sp.dma_start(stagew[:, m, :, :], w.rearrange("(t p) n -> p t n", p=P))\
                    .then_inc(w_loaded[m], 16)
            sp.dma_start(stageo, w_out.rearrange("(t p) n -> p t n", p=P)).then_inc(w_loaded[3], 16)
            sp.dma_start(bo[:, :], b_out).then_inc(bo_loaded, 16)
            walk(sp, stages, prologue[1:])
            sp.wait_ge(y_stored, 16 * B + 16)


def arrays(inputs):
    import numpy as np
    a = {n: np.asarray(v) for n, v in inputs.items()}
    ctx, x = a["ctx_2048"], a["x"]
    kv = a["L0_xattn_kv_w"].reshape(512, 512, 2)
    kvb = a["L0_xattn_kv_b"].reshape(512, 2)
    b_qkv = np.stack([a["L0_xattn_q_b"], kvb[:, 0], kvb[:, 1]]).reshape(3, 4, 128).transpose(2, 0, 1)
    out = {
        "latents": x, "ctx": ctx, "mask": a["mask_BxS2_ik0"],
        "hT": np.concatenate([ctx.transpose(0, 2, 1), x.transpose(0, 2, 1)], axis=2),
        "wq0": a["L0_xattn_q_w"], "wk0": kv[:, :, 0], "wv0": kv[:, :, 1], "wo0": a["L0_xattn_out_w"],
        "b_qkv": b_qkv, "b_out": a["L0_xattn_out_b"].reshape(1, 512),
        "norm_w": a["L0_xattn_postnorm_w"].reshape(4, 128).T,
        "w1": a["L0_xattn_mlp_w1"], "b1": a["L0_xattn_mlp_b1"].reshape(16, 128).T,
        "w2": a["L0_xattn_mlp_w2"], "b2": a["L0_xattn_mlp_b2"].reshape(1, 512),
    }
    for m in "qkv":
        out["w%s1" % m] = a["L1_xattn_W" + m].T
    out["wo1"] = a["L1_xattn_Wo"].T.reshape(2, 2, 4, 16, 256).transpose(0, 2, 1, 3, 4).reshape(256, 256)
    out["bo1"] = a["L1_xattn_bo"].reshape(2, 128).T
    return {n: np.ascontiguousarray(v) for n, v in out.items()}


def program(nc, aps):
    shape = tuple(aps["latents"].shape)
    y = nc.dram_tensor("y", shape, F32, kind="ExternalOutput").ap()
    y_mid = nc.dram_tensor("y_mid", shape, F32, kind="Internal").ap()
    y_mlp = nc.dram_tensor("y_mlp", shape, F32, kind="Internal").ap()
    with nc.psum_tensor("ps", [P, 8, BANK], F32) as psum:
        attention0(nc, psum, aps["latents"], aps["hT"], aps["mask"], aps["wq0"], aps["wk0"], aps["wv0"],
                   aps["wo0"], aps["b_qkv"], aps["b_out"], y_mid)
        mlp(nc, psum, y_mid, aps["latents"], aps["w1"], aps["w2"], aps["b1"], aps["b2"], aps["norm_w"],
            y_mlp)
        attention1(nc, psum, y_mlp, aps["ctx"], aps["wq1"], aps["wk1"], aps["wv1"], aps["wo1"],
                   aps["bo1"], y)


def kernel(**inputs):
    import concourse.bacc as bacc
    from concourse.bass_utils import run_bass_kernel_spmd

    nc = bacc.Bacc("TRN2", target_bir_lowering=False, num_devices=1)
    arr = arrays(inputs)
    aps = {name: nc.dram_tensor(name, v.shape, mybir.dt.from_np(v.dtype), kind="ExternalInput").ap()
           for name, v in arr.items()}
    program(nc, aps)
    return run_bass_kernel_spmd(nc, [arr], core_ids=[0]).results[0]["y"]
```
